# Optimizing a Trainium2 kernel written in Bass

```python
import numpy as np
import jax
import jax.numpy as jnp

def _softmax(x, axis=-1):
    return jax.nn.softmax(x, axis=axis)

def _gelu(x):
    return jax.nn.gelu(x, approximate=True)

def _silu(x):
    return jax.nn.silu(x)

def _sigmoid(x):
    return jax.nn.sigmoid(x)

def _layernorm(x, axis=-1, eps=1e-05):
    m = jnp.mean(x, axis=axis, keepdims=True)
    v = jnp.var(x, axis=axis, keepdims=True)
    return (x - m) / jnp.sqrt(v + eps)

def _scatter_add(tgt, idx, src, axis=0):
    return tgt.at[idx].add(src)

def _segment_sum(src, seg, n):
    return jax.ops.segment_sum(src, seg, n)
kernel_name = 'mk_seq_preln_d1_jaxref_r8_712398'

def setup_inputs(seed: int=0):
    np.random.seed(seed)
    _w = jnp.asarray

    def _L0_attn_setup():
        import jax, jax.numpy as jnp
        import numpy as np
        HIDDEN = 128
        NUM_HEADS = 16
        HEAD = HIDDEN // NUM_HEADS
        LEFT = 64
        RIGHT = 8
        NUM_POS = LEFT + RIGHT + 1
        key = jax.random.key(seed)
        ks = jax.random.split(key, 10)
        s = 1.0 / np.sqrt(HIDDEN)
        return {'hidden_states': jax.random.normal(ks[0], (4, 256, HIDDEN), jnp.float32), 'Wq': jax.random.normal(ks[1], (HIDDEN, HIDDEN), jnp.float32) * s, 'bq': jax.random.normal(ks[2], (HIDDEN,), jnp.float32) * 0.01, 'Wk': jax.random.normal(ks[3], (HIDDEN, HIDDEN), jnp.float32) * s, 'bk': jax.random.normal(ks[4], (HIDDEN,), jnp.float32) * 0.01, 'Wv': jax.random.normal(ks[5], (HIDDEN, HIDDEN), jnp.float32) * s, 'bv': jax.random.normal(ks[6], (HIDDEN,), jnp.float32) * 0.01, 'Wo': jax.random.normal(ks[7], (HIDDEN, HIDDEN), jnp.float32) * s, 'bo': jax.random.normal(ks[8], (HIDDEN,), jnp.float32) * 0.01, 'dist_emb': jax.random.normal(ks[9], (NUM_POS, HEAD), jnp.float32)}
    _L0_attn_in = _L0_attn_setup()

    def _L0_ffn_setup():
        import jax, jax.numpy as jnp
        import numpy as np
        B, S, H, I, E = (2, 512, 128, 64, 8)
        key = jax.random.key(seed)
        ks = jax.random.split(key, 5)
        scale_h = 1.0 / np.sqrt(H)
        scale_i = 1.0 / np.sqrt(I)
        return {'hidden_states': jax.random.normal(ks[0], (B, S, H), dtype=jnp.float32), 'gate_w': jax.random.normal(ks[1], (E, H), dtype=jnp.float32) * scale_h, 'w_gate': jax.random.normal(ks[2], (E, I, H), dtype=jnp.float32) * scale_h, 'w_up': jax.random.normal(ks[3], (E, I, H), dtype=jnp.float32) * scale_h, 'w_down': jax.random.normal(ks[4], (E, H, I), dtype=jnp.float32) * scale_i}
    _L0_ffn_in = _L0_ffn_setup()
    _d = {'L0_attn_hidden_states': _L0_attn_in['hidden_states'], 'L0_attn_Wq': _L0_attn_in['Wq'], 'L0_attn_bq': _L0_attn_in['bq'], 'L0_attn_Wk': _L0_attn_in['Wk'], 'L0_attn_bk': _L0_attn_in['bk'], 'L0_attn_Wv': _L0_attn_in['Wv'], 'L0_attn_bv': _L0_attn_in['bv'], 'L0_attn_Wo': _L0_attn_in['Wo'], 'L0_attn_bo': _L0_attn_in['bo'], 'L0_attn_dist_emb': _L0_attn_in['dist_emb'], 'L0_ffn_gate_w': _L0_ffn_in['gate_w'], 'L0_ffn_w_gate': _L0_ffn_in['w_gate'], 'L0_ffn_w_up': _L0_ffn_in['w_up'], 'L0_ffn_w_down': _L0_ffn_in['w_down']}
    _x0 = _d['L0_attn_hidden_states']
    _d['L0_attn_hidden_states'] = jax.random.normal(jax.random.fold_in(jax.random.key(seed), 1), (16, 256, 128), dtype=_x0.dtype)
    del _x0
    return _d

def reference(L0_attn_hidden_states, L0_attn_Wq, L0_attn_bq, L0_attn_Wk, L0_attn_bk, L0_attn_Wv, L0_attn_bv, L0_attn_Wo, L0_attn_bo, L0_attn_dist_emb, L0_ffn_gate_w, L0_ffn_w_gate, L0_ffn_w_up, L0_ffn_w_down):

    def _L0_attn_ref(hidden_states, Wq, bq, Wk, bk, Wv, bv, Wo, bo, dist_emb):
        import jax, jax.numpy as jnp
        import numpy as np
        HIDDEN = 128
        NUM_HEADS = 16
        HEAD = HIDDEN // NUM_HEADS
        LEFT = 64
        RIGHT = 8
        NUM_POS = LEFT + RIGHT + 1
        B, L, H = hidden_states.shape
        scale = 1.0 / np.sqrt(HEAD)

        def proj(W, b):
            return (hidden_states @ W.T + b).reshape(B, L, NUM_HEADS, HEAD).transpose(0, 2, 1, 3)
        q = proj(Wq, bq)
        k = proj(Wk, bk)
        v = proj(Wv, bv)
        attn = jnp.einsum('bhld,bhrd->bhlr', q, k) * scale
        dist = jnp.arange(L)[None, :] - jnp.arange(L)[:, None]
        dist = jnp.clip(dist, -LEFT, RIGHT) + LEFT
        pos_emb = dist_emb[dist]
        rel = jnp.einsum('bhld,lrd->bhlr', q, pos_emb) * scale
        attn = jax.nn.softmax(attn + rel, axis=-1)
        out = jnp.einsum('bhlr,bhrd->bhld', attn, v)
        out = out.transpose(0, 2, 1, 3).reshape(B, L, H)
        return out @ Wo.T + bo

    def _L0_ffn_ref(hidden_states, gate_w, w_gate, w_up, w_down):
        import jax, jax.numpy as jnp
        import numpy as np
        B, S, H, I, E = (2, 512, 128, 64, 8)
        b, s, h = hidden_states.shape
        x = hidden_states.reshape(-1, h)
        logits = x @ gate_w.T
        top_v = jnp.max(logits, axis=-1)
        sel = jnp.argmax(logits, axis=-1)
        rw = jax.nn.sigmoid(top_v)
        out = jnp.zeros_like(x)
        n_exp = gate_w.shape[0]
        for e in range(n_exp):
            mask = (sel == e).astype(x.dtype)
            xs = x * (rw * mask)[:, None]
            g = xs @ w_gate[e].T
            u = xs @ w_up[e].T
            out = out + u * jax.nn.silu(g) @ w_down[e].T
        return out.reshape(b, s, h)
    x = L0_attn_hidden_states
    x = x + _L0_attn_ref(_layernorm(x, axis=-1), L0_attn_Wq, L0_attn_bq, L0_attn_Wk, L0_attn_bk, L0_attn_Wv, L0_attn_bv, L0_attn_Wo, L0_attn_bo, L0_attn_dist_emb)
    x = x + _L0_ffn_ref(_layernorm(x, axis=-1), L0_ffn_gate_w, L0_ffn_w_gate, L0_ffn_w_up, L0_ffn_w_down)
    return x

_drawn_inputs = setup_inputs


def setup_inputs(seed=0):
    import zlib

    import numpy as np

    out = dict(_drawn_inputs(seed))
    spreads = {}
    factors = {'L0_attn_bq': 6.457, 'L0_attn_bk': 8.0}
    for name, (base, spread) in spreads.items():
        noise = np.random.default_rng([zlib.crc32(name.encode()), seed]).standard_normal(out[name].shape)
        drawn = base * np.exp(spread * noise) if base else spread * noise
        out[name] = jnp.asarray(drawn.astype(out[name].dtype))
    for name, factor in factors.items():
        out[name] = (out[name] * factor).astype(out[name].dtype)
    return out
```

```python
from contextlib import ExitStack

import concourse.bass as bass
from concourse import mybir

ALU = mybir.AluOpType
ACT = mybir.ActivationFunctionType
F32 = mybir.dt.float32
F16 = mybir.dt.float16
AX_X = mybir.AxisListType.X

P = 128
NB = 16
L = 256
D = 128
NH = 16
C = 8
LEFT, RIGHT = 64, 8
NE = 8
NI = 64
NT = L // P
NG = 4
NCH = 16
QR = 32
SCALE = float(C) ** -0.5
EPS = 1e-5
MSCALE = 64.0
XOFF = L - 4
TZW = XOFF + L
WQ, WK, WV, WO, WG = 0, 128, 256, 384, 512
WGU = WG + NE
WD = WGU + NE * 2 * NI
WALL = WD + (NE // 2) * D
MAX_OF_STEP = [0, 0, 0, 0, 0, 2, 2, 2, 2, 2, 2, 2, 2, 0, 0, 0]


class Batch:

    def __init__(self, trip, off):
        self.trip, self.off = trip, off
        self.par = off % 2
        self.fixed = isinstance(trip, int)

    @property
    def b(self):
        return self.trip * 2 + self.off

    def there(self):
        return not self.fixed or 0 <= self.b < NB

    def by(self, n):
        return Batch(self.trip, self.off + n)

    def count(self, per, k):
        n = self.trip * (2 * per) + (per * self.off + k)
        return None if self.fixed and (n <= 0 or self.b >= NB) else n

    def half(self, per, k):
        return self.trip * per + (per * (self.off // 2) + k) if self.there() else None


def build(nc, x, w_all, biases, b_rows, dist_t, dist0, ident16, ident32, sel, kbias, restrow, iota, turned_q, out):
    with ExitStack() as ctx:
        def sb(name, shape, dt):
            return ctx.enter_context(nc.sbuf_tensor(name, shape, dt))

        def ps(name):
            return ctx.enter_context(nc.psum_tensor(name, [P, 512], F32))

        def sem(name):
            return ctx.enter_context(nc.semaphore(name))

        WF = sb("WF", [P, WALL], F32)
        W16 = sb("W16", [P, 2, WALL], F16)
        BI = sb("BI", [P, 2], F32)
        BR = sb("BR", [P, 2, D], F32)
        TF = sb("TF", [P, TZW], F32)
        TH = sb("TH", [P, TZW], F16)
        TZ = sb("TZ", [P, TZW], F16)
        D0 = sb("D0", [P, 1], F32)
        I16 = sb("I16", [P, P], F16)
        I32 = sb("I32", [P, P], F32)
        SEL = sb("SEL", [P, 4, NG, P], F16)
        KB = sb("KB", [P, 1], F32)
        RESTROW = sb("RESTROW", [P, 1], F32)
        IOTA = sb("IOTA", [P, NT, NE], F32)
        XF = [sb(f"XF{p}", [P, NT, D], F32) for p in range(2)]
        ST1 = sb("ST1", [P, NT, 6], F32)
        MV1 = sb("MV1", [P, NT, 2], F32)
        VE1 = sb("VE1", [P, NT, 1], F32)
        HALF = sb("HALF", [P, NT, 1], F32)
        RS1 = sb("RS1", [P, NT, 1], F32)
        XNF = sb("XNF", [P, NT, D], F32)
        XN = sb("XN", [P, 2, NT, D], F16)
        XT = sb("XT", [P, 2, L], F16)
        QKF = sb("QKF", [P, 2, L], F32)
        QK16 = sb("QK16", [P, 2, 2, L], F16)
        QD = sb("QD", [P, NG, L], F16)
        QP = sb("QP", [P, 4, NG, L // 4], F16)
        K4 = [sb(f"K4{p}", [P, NG, L], F16) for p in range(2)]
        Z = [sb(f"Z{p}", [P, 4, NG, L], F16) for p in range(2)]
        R = [sb(f"R{p}", [P, 4, NH, L // 4], F16) for p in range(2)]
        VS = [sb(f"VS{p}", [P, NT, NH, QR], F32) for p in range(2)]
        MXR = sb("MXR", [P, NT, P], F32)
        MXC = sb("MXC", [P, P], F32)
        MN = sb("MN", [P, QR], F32)
        M16 = sb("M16", [P, QR], F16)
        PT = [sb(f"PT{p}", [P, NT, NH, L], F32) for p in range(2)]
        OT = sb("OT", [P, NG, 8, QR], F32)
        RD = sb("RD", [P, NG, 8], F32)
        ON = sb("ON", [P, 8, NG, C], F32)
        OC = sb("OC", [P, L], F32)
        OC16 = sb("OC16", [P, 2, L], F16)
        XB = [sb(f"XB{p}", [P, NT, D], F32) for p in range(2)]
        XBB = sb("XBB", [P, NT, D], F32)
        X2 = [sb(f"X2{p}", [P, NT, D], F32) for p in range(2)]
        ST2 = sb("ST2", [P, NT, 6], F32)
        MV2 = sb("MV2", [P, NT, 2], F32)
        VE2 = sb("VE2", [P, NT, 1], F32)
        RS2 = sb("RS2", [P, NT, 1], F32)
        X2F = sb("X2F", [P, NT, D], F32)
        X2N = sb("X2N", [P, 2, NT, D], F16)
        X2T = sb("X2T", [P, 2, L], F16)
        LMX = sb("LMX", [P, NT], F32)
        LLT = sb("LLT", [P, NT, NE], F32)
        LIX = sb("LIX", [P, NT, NE], F32)
        LID = sb("LID", [P, NT], F32)
        MSK = sb("MSK", [P, NT, NE], F16)
        REX = sb("REX", [P, NT], F32)
        RP1 = sb("RP1", [P, NT], F32)
        RW = sb("RW", [P, NT], F32)
        MK = sb("MK", [P, NE, L], F16)
        XM = sb("XM", [P, 2, NE, L], F16)
        GUF = sb("GUF", [P, NT, 2, NI], F32)
        GE = sb("GE", [P, NT, NI], F32)
        GP = sb("GP", [P, NT, NI], F32)
        GR = sb("GR", [P, NT, NI], F32)
        GS = sb("GS", [P, NT, NI], F32)
        HF = sb("HF", [P, NT, NI], F32)
        H16 = sb("H16", [P, 2, NT, 2, NI], F16)
        HT = sb("HT", [P, 2, L], F16)
        HM = sb("HM", [P, 2, NE // 2, L], F16)
        Y = [sb(f"Y{p}", [P, NT, D], F32) for p in range(2)]

        MX = [ps("MX0"), ps("MX1")]
        SC = [ps("SC0"), ps("SC1")]
        PO = ps("PO")
        BA, BB, BC = ps("BA"), ps("BB"), ps("BC")

        s_cst = sem("s_cst")
        s_wld = sem("s_wld")
        s_zero = sem("s_zero")
        s_w16 = sem("s_w16")
        s_tz = sem("s_tz")
        s_half = sem("s_half")
        s_apart = sem("s_apart")
        s_xf = [sem(f"s_xf{p}") for p in range(2)]
        s_xb = [sem(f"s_xb{p}") for p in range(2)]
        s_z = [sem(f"s_z{p}") for p in range(2)]
        s_r = [sem(f"s_r{p}") for p in range(2)]
        s_qpd = [sem(f"s_qpd{p}") for p in range(2)]
        s_m = [sem(f"s_m{p}") for p in range(2)]
        s_y = [sem(f"s_y{p}") for p in range(2)]
        names = ("ln1 rs1 xnf xn xt_full xt qk_full qk qk16 selk_full k4 selq_full qd qp v_full v mx_full tr mxc "
                 "mt_full m16 sc_full exp pv_full ot on oc16 xbb wo_full x2 ln2 rs2 x2f x2n x2t_full x2t lg_full "
                 "gate rex mk_full mk xm gu_full guf ge h h16 ht_full ht hm dn_full yf").split()
        S = {n: sem("s_" + n) for n in names}
        (s_ln1, s_rs1, s_xnf, s_xn, s_xt_full, s_xt, s_qk_full, s_qk, s_qk16, s_selk_full, s_k4, s_selq_full, s_qd,
         s_qp, s_v_full, s_v, s_mx_full, s_tr, s_mxc, s_mt_full, s_m16, s_sc_full, s_exp, s_pv_full,
         s_ot, s_on, s_oc16, s_xbb, s_wo_full, s_x2, s_ln2, s_rs2, s_x2f, s_x2n, s_x2t_full, s_x2t, s_lg_full,
         s_gate, s_rex, s_mk_full, s_mk, s_xm, s_gu_full, s_guf, s_ge, s_h, s_h16, s_ht_full, s_ht,
         s_hm, s_dn_full, s_yf) = [S[n] for n in names]

        def apart(eng, bt):
            if not bt.fixed:
                eng.sem_inc(s_apart, 1)

        def run(eng, step_all):
            for i in range(-2, 4):
                step_all(i // 2, i % 2)
            with eng.Fori(2, 6) as trip:
                for u in range(2):
                    step_all(trip, u)
            for i in range(12, 18):
                step_all(i // 2, i % 2)

        block = ctx.enter_context(nc.Block())

        @block.sync
        def _(sp):
            def load_xf(bt):
                if not bt.there():
                    return
                prev = Batch(bt.trip, bt.off - 2)
                if (due := prev.count(2, 2)) is not None:
                    sp.wait_ge(s_xnf, due)
                apart(sp, bt)
                sp.dma_start(XF[bt.par][:, :, :], x[bass.ds(bt.b, 1), :, :].rearrange(
                    "o (t p) d -> p (o t) d", p=P)).then_inc(s_xf[bt.par], 16)

            def load_xb(bt):
                if not bt.there():
                    return
                if (due := bt.by(-2).count(1, 1)) is not None:
                    sp.wait_ge(s_xbb, due)
                apart(sp, bt)
                sp.dma_start(XB[bt.par][:, :, :], x[bass.ds(bt.b, 1), :, :].rearrange(
                    "o (t p) d -> p (o t) d", p=P)).then_inc(s_xb[bt.par], 16)

            for dst, src in ((I16, ident16), (SEL, sel), (KB, kbias), (BI, biases), (BR, b_rows)):
                sp.dma_start(dst[:], src).then_inc(s_cst, 16)
            sp.dma_start(WF[:, :], w_all).then_inc(s_wld, 16)
            for dst, src in ((TF, dist_t), (D0, dist0), (RESTROW, restrow), (I32, ident32), (IOTA, iota)):
                sp.dma_start(dst[:], src).then_inc(s_wld, 16)
            load_xf(Batch(0, 0))
            load_xf(Batch(0, 1))

            def step_all(trip, u):
                nxt, last, cur, nxt3 = Batch(trip, u + 1), Batch(trip, u - 1), Batch(trip, u), Batch(trip, u + 3)
                if nxt.there():
                    if (due := last.count(NCH, NCH)) is not None:
                        sp.wait_ge(s_sc_full, due)
                        apart(sp, nxt)
                    if nxt.fixed and nxt.b < 2:
                        sp.wait_ge(s_zero, 4)
                    sp.wait_ge(s_qpd[nxt.par], nxt.half(16, 16))
                    apart(sp, nxt)
                    for a in range(4):
                        sp.dma_start(R[nxt.par][32 * a:32 * a + 32, a, :, :].rearrange(
                            "p (j g) q -> p j (g q)", j=4),
                            turned_q[nxt.par, a].rearrange("(j p) x -> p j x", j=4)).then_inc(s_r[nxt.par], 16)
                    sp.wait_ge(s_qd, nxt.count(2, 2))
                    apart(sp, nxt)
                    for j in range(4):
                        q = slice(32 * j, 32 * j + 32)
                        sp.dma_start(Z[nxt.par][q, j, :, :], QD[q, :, :]).then_inc(s_z[nxt.par], 16)
                if nxt3.there() and not (nxt3.fixed and nxt3.b < 2):
                    load_xf(nxt3)
                if cur.there():
                    load_xb(cur)
                late = Batch(trip, u - 2)
                if late.there():
                    sp.wait_ge(s_yf, late.count(1, 1))
                    apart(sp, late)
                    sp.dma_start(out[bass.ds(late.b, 1), :, :].rearrange("o (t p) d -> p (o t) d", p=P),
                                 Y[late.par][:, :, :]).then_inc(s_y[late.par], 16)
                nxt2 = Batch(trip, u + 2)
                if nxt2.there():
                    if (due := nxt2.by(-2).half(64, 64)) is not None:
                        sp.wait_ge(s_r[nxt2.par], due)
                        apart(sp, nxt2)
                    sp.wait_ge(s_qp, nxt2.count(2, 2))
                    apart(sp, nxt2)
                    sp.dma_start(turned_q[nxt2.par].rearrange("a p x -> p a x"),
                                 QP[:, :, :, :].rearrange("p a g q -> p a (g q)")).then_inc(s_qpd[nxt2.par], 16)
                if nxt.there():
                    sp.wait_ge(s_m16, nxt.count(2, 2))
                    apart(sp, nxt)
                    sp.wait_ge(s_z[nxt.par], nxt.half(64, 64))
                    for j in range(4):
                        row = 32 * j + 3 * C
                        sp.dma_start(Z[nxt.par][row:row + 1, j, :, :].rearrange("o g (b l) -> o (g b) l", l=QR),
                                     M16[32 * j:32 * j + 32, :]).then_inc(s_m[nxt.par], 16)

            run(sp, step_all)
            for par in range(2):
                sp.wait_ge(s_y[par], 16 * NB // 2)

        @block.tensor
        def _(pe):
            mm = nc.tensor.matmul

            def three(out_ap, stat, mov, start, stop):
                mm(out_ap, stat(0), mov(0), start=start, stop=False, skip_group_check=True)
                mm(out_ap, stat(0), mov(1), start=False, stop=False, skip_group_check=True)
                return mm(out_ap, stat(1), mov(0), start=False, stop=stop, skip_group_check=True)

            def chunk(bank, bt, n):
                lb, rt = n // 2, n % 2
                groups = [q for q in range(8 * lb, 8 * lb + 8)
                          if not (rt + 1) * P - 1 <= 4 * q - LEFT]
                for g in range(NG):
                    last = mm(bank[:, P * g:P * g + P], K4[bt.par][:, g, P * rt:P * rt + P],
                              Z[bt.par][:, :, g, QR * lb:QR * lb + QR],
                              start=g == 0, stop=g == NG - 1 and not groups, skip_group_check=True)
                outs = bank[:, :].rearrange("p (g j q a) -> p g j q a", g=NG, j=4, a=4)
                rel = R[bt.par][:, :, :, :].rearrange("p a (j g) q -> p g j a q", j=4)
                for q in groups:
                    at = XOFF + P * rt - 4 * q
                    last = mm(outs[:, :, :, q - 8 * lb, :], TZ[:, at:at + P], rel[:, :, :, :, q],
                              start=False, stop=q == groups[-1], skip_group_check=True)
                return last

            def max_chunk(bt, n):
                if n == 0:
                    pe.wait_ge(s_z[bt.par], bt.half(64, 64))
                    pe.wait_ge(s_r[bt.par], bt.half(64, 64))
                    pe.wait_ge(s_k4, bt.count(2, 2))
                    if bt.fixed and bt.b == 0:
                        pe.wait_ge(s_tz, 3)
                if (due := bt.count(NCH, n - 1)) is not None:
                    pe.wait_ge(s_tr, due)
                chunk(MX[n % 2], bt, n).then_inc(s_mx_full, 1)

            def score_chunk(bt, n):
                if n == 0:
                    pe.wait_ge(s_m[bt.par], bt.half(64, 64))
                if (due := bt.count(NCH, n - 1)) is not None:
                    pe.wait_ge(s_exp, due)
                chunk(SC[n % 2], bt, n).then_inc(s_sc_full, 1)

            def select(bank, kind, g0, full):
                for g in (g0, g0 + 1):
                    o = bank[:, L * (g - g0):L * (g - g0) + L]
                    mm(o, SEL[:, 2 * kind, g, :], QK16[:, 0, kind, :], start=True, stop=False)
                    last = mm(o, SEL[:, 2 * kind + 1, g, :], QK16[:, 1, kind, :], start=False, stop=True)
                last.then_inc(full, 1)

            def keys(bt):
                if not bt.there():
                    return
                pe.wait_ge(s_qk16, bt.count(2, 2))
                pe.wait_ge(s_qd, bt.count(2, 2))
                if (due := bt.by(-1).count(2, 1)) is not None:
                    pe.wait_ge(s_m16, due)
                if (due := bt.by(-3).count(1, 1)) is not None:
                    pe.wait_ge(s_guf, due)
                select(BA, 1, 0, s_selk_full)
                if (due := bt.by(-3).count(4, 4)) is not None:
                    pe.wait_ge(s_mk, due)
                select(BC, 1, 2, s_selk_full)

            def pv(bt, half):
                if not bt.there():
                    return
                if half == 0:
                    pe.wait_ge(s_v, bt.count(1, 1))
                    pe.wait_ge(s_exp, bt.count(NCH, NCH))
                if (due := bt.count(2, half)) is not None:
                    pe.wait_ge(s_ot, due)
                for gg in range(2):
                    for rt in range(NT):
                        for j in range(4):
                            h = 4 * (2 * half + gg) + j
                            last = mm(PO[32 * j:32 * j + 32, L * gg:L * gg + L], VS[bt.par][:, rt, h, :],
                                      PT[bt.par][:, rt, h, :], start=rt == 0, stop=rt == NT - 1,
                                      skip_group_check=True)
                last.then_inc(s_pv_full, 1)

            def values(bt):
                if not bt.there():
                    return
                pe.wait_ge(s_k4, bt.count(2, 2))
                for t in range(NT):
                    last = three(BC[:, D * t:D * t + D], lambda s: XT[:, s, P * t:P * t + P],
                                 lambda s: W16[:, s, WV:WV + D], True, True)
                last.then_inc(s_v_full, 1)

            def turn(bank, src, full):
                o = bank[:, 0:2 * P].bitcast(F16)
                for s in range(2):
                    for t in range(NT):
                        c = (s * NT + t) * P
                        last = nc.tensor.transpose(o[:, c:c + P], src(s, t), I16[:, :])
                last.then_inc(full, 1)

            def h_turn(bt):
                if not bt.there():
                    return
                pe.wait_ge(s_h16, bt.count(2, 2))
                pe.wait_ge(s_mk, bt.count(4, 4))
                turn(BB, lambda s, t: H16[:, s, t, :, :].rearrange("p a i -> p (a i)"), s_ht_full)

            def x_turn(bt):
                if not bt.there():
                    return
                pe.wait_ge(s_xn, bt.count(2, 2))
                if (due := bt.by(-1).count(2, 1)) is not None:
                    pe.wait_ge(s_k4, due)
                turn(BA, lambda s, t: XN[:, s, t, :], s_xt_full)

            def project_out(bt):
                if not bt.there():
                    return
                pe.wait_ge(s_oc16, bt.count(2, 2))
                if (due := bt.by(-1).count(1, 1)) is not None:
                    pe.wait_ge(s_ht, due)
                for t in range(NT):
                    last = three(BB[:, D * t:D * t + D], lambda s: OC16[:, s, P * t:P * t + P],
                                 lambda s: W16[:, s, WO:WO + D], True, True)
                last.then_inc(s_wo_full, 1)

            def project_qk(bt):
                if not bt.there():
                    return
                pe.wait_ge(s_xt, bt.count(1, 1))
                for kind, w in enumerate((WQ, WK)):
                    last = three(BA[:, L * kind:L * kind + L], lambda s: W16[:, s, w:w + D],
                                 lambda s: XT[:, s, :], True, True)
                last.then_inc(s_qk_full, 1)

            def down(bt):
                if not bt.there():
                    return
                pe.wait_ge(s_hm, bt.count(2, 2))
                if (due := bt.by(1).count(1, 1)) is not None:
                    pe.wait_ge(s_x2, due)
                for t in range(NT):
                    for e in range(NE // 2):
                        last = three(BB[:, D * t:D * t + D], lambda s: HM[:, s, e, P * t:P * t + P],
                                     lambda s: W16[:, s, WD + D * e:WD + D * e + D], e == 0, e == NE // 2 - 1)
                last.then_inc(s_dn_full, 1)

            def x2_turn(bt):
                if not bt.there():
                    return
                pe.wait_ge(s_x2n, bt.count(2, 2))
                if (due := bt.by(2).count(1, 1)) is not None:
                    pe.wait_ge(s_v, due)
                turn(BC, lambda s, t: X2N[:, s, t, :], s_x2t_full)

            def queries(bt, half):
                if not bt.there():
                    return
                if half == 0:
                    pe.wait_ge(s_qk16, bt.count(2, 2))
                    select(BA, 0, 0, s_selq_full)
                else:
                    if (due := bt.by(-1).count(1, 1)) is not None:
                        pe.wait_ge(s_v, due)
                    if (due := bt.by(-3).count(1, 1)) is not None:
                        pe.wait_ge(s_x2t, due)
                    select(BC, 0, 2, s_selq_full)

            def logits(bt):
                if not bt.there():
                    return
                pe.wait_ge(s_x2t, bt.count(1, 1))
                if (due := bt.by(-1).count(1, 1)) is not None:
                    pe.wait_ge(s_yf, due)
                for t in range(NT):
                    last = three(BB[:, NE * t:NE * t + NE], lambda s: X2T[:, s, P * t:P * t + P],
                                 lambda s: W16[:, s, WG:WG + NE], True, True)
                last.then_inc(s_lg_full, 1)

            def max_turn(bt):
                if not bt.there():
                    return
                pe.wait_ge(s_mxc, bt.count(1, 1))
                if (due := bt.by(1).count(2, 1)) is not None:
                    pe.wait_ge(s_qd, due)
                nc.tensor.transpose(BA[:, 0:P], MXC[:, :], I32[:, :]).then_inc(s_mt_full, 1)

            def masks(bt, n):
                if not bt.there():
                    return
                if n == 0:
                    pe.wait_ge(s_gate, bt.count(7, 5))
                elif n == 1:
                    if (due := bt.by(3).count(2, 2)) is not None:
                        pe.wait_ge(s_qd, due)
                else:
                    if (due := bt.count(4, n - 1)) is not None:
                        pe.wait_ge(s_mk, due)
                bank = (BB, BC)[n % 2]
                for e in (2 * n, 2 * n + 1):
                    for t in range(NT):
                        c = L * (e - 2 * n) + P * t
                        last = mm(bank[:, c:c + P], MSK[:, t, e:e + 1].to_broadcast([P, P]), I16[:, :],
                                  start=True, stop=True)
                last.then_inc(s_mk_full, 1)

            def gate_up(bt):
                if not bt.there():
                    return
                pe.wait_ge(s_xm, bt.count(2, 2))
                if (due := bt.by(2).count(2, 1)) is not None:
                    pe.wait_ge(s_m16, due)
                for t in range(NT):
                    for e in range(NE):
                        last = three(BA[:, D * t:D * t + D], lambda s: XM[:, s, e, P * t:P * t + P],
                                     lambda s: W16[:, s, WGU + 2 * NI * e:WGU + 2 * NI * (e + 1)],
                                     e == 0, e == NE - 1)
                last.then_inc(s_gu_full, 1)

            pe.wait_ge(s_w16, 2)
            pe.wait_ge(s_cst, 80)
            pe.wait_ge(s_wld, 96)

            def step_all(trip, u):
                i2, i1, i0, m1, m2 = [Batch(trip, u + k) for k in (2, 1, 0, -1, -2)]
                nmax = 0
                for n in range(NCH):
                    if n == 0:
                        keys(i1)
                        pv(m1, 0)
                    if n == 1:
                        pv(m1, 1)
                    if n == 2:
                        values(i1)
                    if n == 3:
                        h_turn(m2)
                    if n == 4:
                        project_out(m1)
                    if n == 5:
                        x_turn(i2)
                    if n == 7:
                        project_qk(i2)
                        down(m2)
                    if n == 8:
                        x2_turn(m1)
                    if n == 9:
                        logits(m1)
                    if n == 10:
                        queries(i2, 0)
                    if n == 11:
                        queries(i2, 1)
                    if n == 12:
                        masks(m1, 0)
                        masks(m1, 1)
                    if n == 13:
                        masks(m1, 2)
                        masks(m1, 3)
                    if n == 14:
                        max_turn(i1)
                    if n == 15:
                        gate_up(m1)
                    if i0.there():
                        score_chunk(i0, n)
                    for _ in range(MAX_OF_STEP[n]):
                        if i1.there():
                            max_chunk(i1, nmax)
                        nmax += 1

            run(pe, step_all)

        @block.scalar
        def _(act):
            copy = nc.scalar.activation

            def exps(bt, n):
                if not bt.there():
                    return
                lb, rt = n // 2, n % 2
                if n == 0:
                    if (due := bt.by(-2).count(2, 2)) is not None:
                        act.wait_ge(s_pv_full, due)
                act.wait_ge(s_sc_full, bt.count(NCH, n + 1))
                copy(PT[bt.par][:, rt, :, QR * lb:QR * lb + QR],
                     SC[n % 2][:, :].rearrange("p (h l) -> p h l", h=NH), ACT.Exp,
                     scale=SCALE).then_inc(s_exp, 1)

            def keys(bt):
                if not bt.there():
                    return
                if (due := bt.by(-2).count(NCH, NCH)) is not None:
                    act.wait_ge(s_sc_full, due)
                for half, bank in enumerate((BA, BC)):
                    act.wait_ge(s_selk_full, bt.count(2, half + 1))
                    copy(K4[bt.par][:, 2 * half:2 * half + 2, :],
                         bank[:, :].rearrange("p (g l) -> p g l", g=2), ACT.Identity,
                         bias=KB[:, 0:1]).then_inc(s_k4, 1)

            def queries(bt, half):
                if not bt.there():
                    return
                if half == 0:
                    if (due := bt.by(-1).half(64, 64)) is not None:
                        act.wait_ge(s_z[1 - bt.par], due)
                    if (due := bt.by(-1).half(16, 16)) is not None:
                        act.wait_ge(s_qpd[1 - bt.par], due)
                act.wait_ge(s_selq_full, bt.count(2, half + 1))
                copy(QP[:, :, 2 * half:2 * half + 2, :],
                     (BA, BC)[half][:, :].rearrange("p (g q a) -> p a g q", g=2, a=4),
                     ACT.Copy).then_inc(s_qp, 1)
                copy(QD[:, 2 * half:2 * half + 2, :],
                     (BA, BC)[half][:, :].rearrange("p (g l) -> p g l", g=2),
                     ACT.Copy).then_inc(s_qd, 1)

            def turned(bt, bank, dst, full, done, user, used):
                if not bt.there():
                    return
                if used is not None:
                    act.wait_ge(user, used)
                act.wait_ge(full, bt.count(1, 1))
                copy(dst[:, :, :], bank[:, 0:2 * P].bitcast(F16).rearrange("p (s l) -> p s l", s=2),
                     ACT.Copy).then_inc(done, 1)

            def qk(bt):
                if not bt.there():
                    return
                if (due := bt.by(-1).count(2, 2)) is not None:
                    act.wait_ge(s_qk16, due)
                act.wait_ge(s_qk_full, bt.count(1, 1))
                for kind in range(2):
                    copy(QKF[:, kind, :], BA[:, L * kind:L * kind + L], ACT.Identity,
                         bias=BI[:, kind:kind + 1]).then_inc(s_qk, 1)

            def masks(bt, n):
                if not bt.there():
                    return
                if n == 0:
                    if (due := bt.by(-1).count(2, 2)) is not None:
                        act.wait_ge(s_hm, due)
                act.wait_ge(s_mk_full, bt.count(4, n + 1))
                copy(MK[:, 2 * n:2 * n + 2, :], (BB, BC)[n % 2][:, :].rearrange("p (e l) -> p e l", e=2),
                     ACT.Copy).then_inc(s_mk, 1)

            def rw_exp(bt):
                if not bt.there():
                    return
                if (due := bt.by(-1).count(7, 6)) is not None:
                    act.wait_ge(s_gate, due)
                act.wait_ge(s_gate, bt.count(7, 1))
                copy(REX[:, :], LMX[:, :], ACT.Exp, scale=-1.0).then_inc(s_rex, 1)

            def gate_exp(bt):
                if not bt.there():
                    return
                if (due := bt.by(-1).count(4, 1)) is not None:
                    act.wait_ge(s_h, due)
                act.wait_ge(s_guf, bt.count(1, 1))
                copy(GE[:, :, :], GUF[:, :, 0, :], ACT.Exp, scale=-1.0).then_inc(s_ge, 1)

            act.wait_ge(s_cst, 80)

            def step_all(trip, u):
                i2, i1, i0, m1, m2 = [Batch(trip, u + k) for k in (2, 1, 0, -1, -2)]
                for n in range(NCH):
                    if n == 0:
                        keys(i1)
                        gate_exp(m2)
                    if n == 3:
                        turned(m2, BB, HT, s_ht_full, s_ht,
                               s_hm, m2.by(-1).count(2, 2))
                    if n == 5:
                        turned(i2, BA, XT, s_xt_full, s_xt,
                               s_v_full, i1.count(1, 1))
                    if n == 7:
                        qk(i2)
                    if n == 8:
                        turned(m1, BC, X2T, s_x2t_full, s_x2t,
                               s_xm, m2.count(2, 2))
                    if n == 10:
                        queries(i2, 0)
                    if n == 11:
                        rw_exp(m1)
                        queries(i2, 1)
                    if n == 12:
                        masks(m1, 0)
                        masks(m1, 1)
                    if n == 13:
                        masks(m1, 2)
                        masks(m1, 3)
                    exps(i0, n)

            run(act, step_all)

        @block.vector
        def _(dve):
            v = nc.vector

            def stats(bt, src, st, mv, done, ready, used):
                ready()
                for t in range(NT):
                    v.bn_stats(st[:, t, :], src[:, t, :]).then_inc(done, 1)
                used()
                for t in range(NT):
                    dve.wait_ge(done, bt.count(4, t + 1))
                    apart(dve, bt)
                    v.bn_aggr(mv[:, t, :], st[:, t, :]).then_inc(done, 1)

            def ln1(bt):
                if not bt.there():
                    return
                before = Batch(bt.trip, bt.off - 1)

                def used():
                    if (due := before.count(2, 2)) is not None:
                        dve.wait_ge(s_xnf, due)

                def ready():
                    if (due := before.count(4, 4)) is not None:
                        dve.wait_ge(s_ln1, due)
                    dve.wait_ge(s_xf[bt.par], bt.half(16, 16))
                stats(bt, XF[bt.par], ST1, MV1, s_ln1, ready, used)

            def normalise(bt, src, mv, rs, full, done):
                for t in range(NT):
                    v.tensor_scalar(full[:, t, :], src[:, t, :], mv[:, t, 0:1], rs[:, t, :],
                                    ALU.subtract, ALU.mult).then_inc(done, 1)

            def norm1(bt):
                if not bt.there():
                    return
                dve.wait_ge(s_rs1, bt.count(2, 2))
                if (due := bt.by(-1).count(2, 2)) is not None:
                    dve.wait_ge(s_xn, due)
                apart(dve, bt)
                normalise(bt, XF[bt.par], MV1, RS1, XNF, s_xnf)

            def norm2(bt):
                if not bt.there():
                    return
                dve.wait_ge(s_rs2, bt.count(2, 2))
                if (due := bt.by(-1).count(2, 2)) is not None:
                    dve.wait_ge(s_x2n, due)
                apart(dve, bt)
                normalise(bt, X2[bt.par], MV2, RS2, X2F, s_x2f)

            def gates_scale(bt):
                if not bt.there():
                    return
                dve.wait_ge(s_gu_full, bt.count(1, 1))
                dve.wait_ge(s_gate, bt.count(7, 7))
                if (due := bt.by(-1).count(1, 1)) is not None:
                    dve.wait_ge(s_ge, due)
                if (due := bt.by(-1).count(4, 4)) is not None:
                    dve.wait_ge(s_h, due)
                v.tensor_tensor(GUF[:, :, :, :].rearrange("p t a i -> p t (a i)"),
                                BA[:, 0:NT * D].rearrange("p (t d) -> p t d", t=NT),
                                RW[:, :].rearrange("p (t o) -> p t o", o=1).to_broadcast([P, NT, D]),
                                ALU.mult).then_inc(s_guf, 1)

            def hidden(bt):
                if not bt.there():
                    return
                dve.wait_ge(s_ge, bt.count(1, 1))
                v.tensor_scalar(GP[:, :, :], GE[:, :, :], 1.0, None, ALU.add).then_inc(s_h, 1)
                dve.wait_ge(s_h, bt.count(4, 1))
                v.reciprocal(GR[:, :, :], GP[:, :, :]).then_inc(s_h, 1)
                dve.wait_ge(s_h, bt.count(4, 2))
                v.tensor_tensor(GS[:, :, :], GUF[:, :, 0, :], GR[:, :, :], ALU.mult).then_inc(s_h, 1)
                dve.wait_ge(s_h, bt.count(4, 3))
                if (due := bt.by(-1).count(2, 2)) is not None:
                    dve.wait_ge(s_h16, due)
                v.tensor_tensor(HF[:, :, :], GS[:, :, :], GUF[:, :, 1, :], ALU.mult).then_inc(s_h, 1)

            def out_turn(bt, half):
                if not bt.there():
                    return
                if half == 0:
                    if (due := bt.by(-1).count(3, 2)) is not None:
                        dve.wait_ge(s_on, due)
                dve.wait_ge(s_pv_full, bt.count(2, half + 1))
                v.transpose(OT[:, 2 * half:2 * half + 2, :, :].rearrange("p g b r -> p (g b r)"),
                            PO[:, :]).then_inc(s_ot, 1)

            def out_norm(bt):
                if not bt.there():
                    return
                dve.wait_ge(s_ot, bt.count(2, 2))
                v.reciprocal(RD[:, :, :], OT[:, :, :, C]).then_inc(s_on, 1)
                dve.wait_ge(s_on, bt.count(3, 1))
                v.tensor_tensor(ON[:, :, :, :].rearrange("p b g c -> p g b c"), OT[:, :, :, 0:C],
                                RD[:, :, :].rearrange("p g (b o) -> p g b o", o=1).to_broadcast([P, NG, 8, C]),
                                ALU.mult).then_inc(s_on, 1)
                dve.wait_ge(s_on, bt.count(3, 2))
                if (due := bt.by(-1).count(2, 2)) is not None:
                    dve.wait_ge(s_oc16, due)
                v.transpose(OC[:, :], ON[:, :, :, :].rearrange("p b g c -> p (b g c)")).then_inc(s_on, 1)

            def values(bt):
                if not bt.there():
                    return
                if bt.fixed and bt.b < 2:
                    dve.wait_ge(s_zero, 6)
                dve.wait_ge(s_v_full, bt.count(1, 1))
                if (due := bt.by(-2).count(2, 2)) is not None:
                    dve.wait_ge(s_pv_full, due)
                v.tensor_tensor(VS[bt.par][:, :, :, 0:C],
                                BC[:, 0:NT * D].rearrange("p (t h c) -> p t h c", t=NT, c=C),
                                BR[:, 0:1, :].rearrange("p o (h c) -> p o h c", c=C)
                                .to_broadcast([P, NT, NH, C]), ALU.add).then_inc(s_v, 1)

            def maxima(bt, n):
                lb, rt = n // 2, n % 2
                if n == 0:
                    if (due := bt.by(-1).count(1, 1)) is not None:
                        dve.wait_ge(s_mxc, due)
                dve.wait_ge(s_mx_full, bt.count(NCH, n + 1))
                v.tensor_reduce(
                    MXR[:, rt, :].rearrange("p (j g b) -> p g j b", j=4, b=8)[:, :, :, lb],
                    MX[n % 2][:, :].rearrange("p (h l) -> p h l", l=QR), axis=AX_X, op=ALU.max,
                    apply_transpose=True).then_inc(s_tr, 1)

            def hidden_mask(bt):
                if not bt.there():
                    return
                dve.wait_ge(s_ht, bt.count(1, 1))
                dve.wait_ge(s_mk, bt.count(4, 4))
                if (due := bt.by(-1).count(1, 1)) is not None:
                    dve.wait_ge(s_dn_full, due)
                for e2 in range(2):
                    q = slice(NI * e2, NI * e2 + NI)
                    mk = MK[q, :, :].rearrange("p (e two) l -> p e two l", two=2)[:, :, e2, :]
                    for s in range(2):
                        last = v.tensor_tensor(HM[q, s, :, :],
                                               HT[q, s:s + 1, :].to_broadcast([NI, NE // 2, L]),
                                               mk, ALU.mult)
                    last.then_inc(s_hm, 1)

            def attended(bt):
                if not bt.there():
                    return
                dve.wait_ge(s_wo_full, bt.count(1, 1))
                dve.wait_ge(s_xbb, bt.count(1, 1))
                if (due := bt.by(-2).count(1, 1)) is not None:
                    dve.wait_ge(s_yf, due)
                v.tensor_tensor(X2[bt.par][:, :, :], BB[:, 0:NT * D].rearrange("p (t d) -> p t d", t=NT),
                                XBB[:, :, :], ALU.add).then_inc(s_x2, 1)
                before = Batch(bt.trip, bt.off - 1)

                def ready():
                    dve.wait_ge(s_x2, bt.count(1, 1))
                    if (due := before.count(4, 4)) is not None:
                        dve.wait_ge(s_ln2, due)

                def used():
                    if (due := before.count(2, 2)) is not None:
                        dve.wait_ge(s_x2f, due)
                stats(bt, X2[bt.par], ST2, MV2, s_ln2, ready, used)

            def result(bt):
                if not bt.there():
                    return
                dve.wait_ge(s_dn_full, bt.count(1, 1))
                prev = Batch(bt.trip, bt.off - 2)
                if (due := prev.half(16, 16)) is not None:
                    dve.wait_ge(s_y[prev.par], due)
                v.tensor_tensor(Y[bt.par][:, :, :], BB[:, 0:NT * D].rearrange("p (t d) -> p t d", t=NT),
                                X2[bt.par][:, :, :], ALU.add).then_inc(s_yf, 1)

            def gate(bt):
                if not bt.there():
                    return
                before = Batch(bt.trip, bt.off - 1)
                lg = BB[:, 0:NT * NE].rearrange("p (t e) -> p t e", t=NT)
                dve.wait_ge(s_lg_full, bt.count(1, 1))
                if (due := before.count(1, 1)) is not None:
                    dve.wait_ge(s_rex, due)
                v.tensor_reduce(LMX[:, :], lg, axis=AX_X, op=ALU.max).then_inc(s_gate, 1)
                dve.wait_ge(s_gate, bt.count(7, 1))
                v.tensor_tensor(LLT[:, :, :], lg,
                                LMX[:, :].rearrange("p (t o) -> p t o", o=1).to_broadcast([P, NT, NE]),
                                ALU.is_lt).then_inc(s_gate, 1)
                dve.wait_ge(s_gate, bt.count(7, 2))
                v.scalar_tensor_tensor(LIX[:, :, :], LLT[:, :, :], float(NE), IOTA[:, :, :],
                                       ALU.mult, ALU.add).then_inc(s_gate, 1)
                dve.wait_ge(s_gate, bt.count(7, 3))
                v.tensor_reduce(LID[:, :], LIX[:, :, :], axis=AX_X, op=ALU.min).then_inc(s_gate, 1)
                dve.wait_ge(s_gate, bt.count(7, 4))
                if (due := before.count(4, 4)) is not None:
                    dve.wait_ge(s_mk_full, due)
                v.tensor_tensor(MSK[:, :, :], IOTA[:, :, :],
                                LID[:, :].rearrange("p (t o) -> p t o", o=1).to_broadcast([P, NT, NE]),
                                ALU.is_equal).then_inc(s_gate, 1)

            def weight(bt):
                if not bt.there():
                    return
                before = Batch(bt.trip, bt.off - 1)
                dve.wait_ge(s_rex, bt.count(1, 1))
                v.tensor_scalar(RP1[:, :], REX[:, :], 1.0, None, ALU.add).then_inc(s_gate, 1)
                dve.wait_ge(s_gate, bt.count(7, 6))
                if (due := before.count(1, 1)) is not None:
                    dve.wait_ge(s_guf, due)
                v.reciprocal(RW[:, :], RP1[:, :]).then_inc(s_gate, 1)

            def max_join(bt):
                if not bt.there():
                    return
                dve.wait_ge(s_tr, bt.count(NCH, NCH))
                if (due := bt.by(-1).count(1, 1)) is not None:
                    dve.wait_ge(s_mt_full, due)
                v.tensor_tensor(MXC[:, :], MXR[:, 0, :], MXR[:, 1, :], ALU.max).then_inc(s_mxc, 1)

            def max_cut(bt):
                if not bt.there():
                    return
                dve.wait_ge(s_mt_full, bt.count(1, 1))
                if (due := bt.by(-1).count(2, 2)) is not None:
                    dve.wait_ge(s_m16, due)
                v.tensor_reduce(MN[:, :], BA[:, 0:P].rearrange("p (q l) -> p l q", q=4), axis=AX_X,
                                op=ALU.max).then_inc(s_m16, 1)
                dve.wait_ge(s_m16, bt.count(2, 1))
                if (due := bt.by(-1).half(64, 64)) is not None:
                    dve.wait_ge(s_m[1 - bt.par], due)
                v.tensor_scalar(M16[:, :], MN[:, :], -1.0 / MSCALE, None, ALU.mult).then_inc(s_m16, 1)

            def rows_mask(bt, half):
                if not bt.there():
                    return
                if half == 0:
                    if (due := bt.by(-1).count(1, 1)) is not None:
                        dve.wait_ge(s_gu_full, due)
                dve.wait_ge(s_x2t, bt.count(1, 1))
                dve.wait_ge(s_mk, bt.count(4, 2 * half + 2))
                e = slice(4 * half, 4 * half + 4)
                for s in range(2):
                    last = v.tensor_tensor(XM[:, s, e, :], X2T[:, s:s + 1, :].to_broadcast([P, 4, L]),
                                           MK[:, e, :], ALU.mult)
                last.then_inc(s_xm, 1)

            for p in range(2):
                v.memset(Z[p][:], 0.0).then_inc(s_zero, 1)
                v.memset(R[p][:], 0.0).then_inc(s_zero, 1)
            for p in range(2):
                v.memset(VS[p][:], 1.0).then_inc(s_zero, 1)
            dve.wait_ge(s_wld, 96)
            v.tensor_copy(W16[:, 0, :], WF[:, :]).then_inc(s_w16, 1)
            dve.wait_ge(s_w16, 1)
            v.tensor_tensor(W16[:, 1, :], WF[:, :], W16[:, 0, :], ALU.subtract).then_inc(s_w16, 1)
            v.tensor_scalar(TF[:, :], TF[:, :], D0[:, 0:1], None, ALU.subtract).then_inc(s_tz, 1)
            dve.wait_ge(s_tz, 1)
            v.tensor_copy(TH[:, :], TF[:, :]).then_inc(s_tz, 1)
            dve.wait_ge(s_tz, 2)
            v.scalar_tensor_tensor(TZ[:, :], TH[:, :], RESTROW[:, 0:1], TF[:, :],
                                   ALU.mult, ALU.add).then_inc(s_tz, 1)

            def step_all(trip, u):
                i2, i1, i0, m1, m2 = [Batch(trip, u + k) for k in (2, 1, 0, -1, -2)]
                nmax = 0
                for n in range(NCH):
                    if n == 0:
                        gates_scale(m2)
                        ln1(i2)
                        out_turn(m1, 0)
                    if n == 1:
                        hidden(m2)
                        norm1(i2)
                        out_turn(m1, 1)
                        out_norm(m1)
                    if n == 3:
                        values(i1)
                    if n == 4:
                        hidden_mask(m2)
                    if n == 5:
                        attended(m1)
                    if n == 6:
                        norm2(m1)
                    if n == 8:
                        result(m2)
                    if n == 10:
                        gate(m1)
                    if n == 12:
                        weight(m1)
                    if n == 13:
                        max_join(i1)
                    if n == 14:
                        max_cut(i1)
                        rows_mask(m1, 0)
                    if n == 15:
                        rows_mask(m1, 1)
                    for _ in range(MAX_OF_STEP[n]):
                        if i1.there():
                            maxima(i1, nmax)
                        nmax += 1

            run(dve, step_all)

        @block.gpsimd
        def _(pool):
            g = nc.gpsimd

            def cut(bt, hi, lo, src, done, per, k):
                apart(pool, bt)
                g.tensor_scalar(hi, src, 1.0, 0.0, ALU.mult, ALU.add).then_inc(done, 1)
                pool.wait_ge(done, bt.count(per, k + 1))
                g.tensor_tensor(lo, src, hi, ALU.subtract).then_inc(done, 1)

            def rstd1(bt):
                if not bt.there():
                    return
                if (due := bt.by(-1).count(2, 2)) is not None:
                    pool.wait_ge(s_rs1, due)
                pool.wait_ge(s_ln1, bt.count(4, 4))
                apart(pool, bt)
                g.tensor_scalar(VE1[:, :, :], MV1[:, :, 1:2], EPS, None, ALU.add).then_inc(s_rs1, 1)
                pool.wait_ge(s_rs1, bt.count(2, 1))
                g.tensor_tensor(RS1[:, :, :], VE1[:, :, :], HALF[:, :, :], ALU.pow).then_inc(s_rs1, 1)

            def rstd2(bt):
                if not bt.there():
                    return
                if (due := bt.by(-1).count(2, 2)) is not None:
                    pool.wait_ge(s_rs2, due)
                pool.wait_ge(s_ln2, bt.count(4, 4))
                apart(pool, bt)
                g.tensor_scalar(VE2[:, :, :], MV2[:, :, 1:2], EPS, None, ALU.add).then_inc(s_rs2, 1)
                pool.wait_ge(s_rs2, bt.count(2, 1))
                g.tensor_tensor(RS2[:, :, :], VE2[:, :, :], HALF[:, :, :], ALU.pow).then_inc(s_rs2, 1)

            def rows1(bt):
                if not bt.there():
                    return
                pool.wait_ge(s_xnf, bt.count(2, 2))
                if (due := bt.by(-1).count(1, 1)) is not None:
                    pool.wait_ge(s_xt_full, due)
                cut(bt, XN[:, 0, :, :], XN[:, 1, :, :], XNF[:, :, :], s_xn, 2, 0)

            def rows2(bt):
                if not bt.there():
                    return
                pool.wait_ge(s_x2f, bt.count(2, 2))
                if (due := bt.by(-1).count(1, 1)) is not None:
                    pool.wait_ge(s_x2t_full, due)
                cut(bt, X2N[:, 0, :, :], X2N[:, 1, :, :], X2F[:, :, :], s_x2n, 2, 0)

            def residual(bt):
                if not bt.there():
                    return
                if (due := bt.by(-1).count(1, 1)) is not None:
                    pool.wait_ge(s_x2, due)
                pool.wait_ge(s_xb[bt.par], bt.half(16, 16))
                g.tensor_tensor(XBB[:, :, :], XB[bt.par][:, :, :], BR[:, 1:2, :].to_broadcast([P, NT, D]),
                                ALU.add).then_inc(s_xbb, 1)

            def hidden(bt):
                if not bt.there():
                    return
                pool.wait_ge(s_h, bt.count(4, 4))
                if (due := bt.by(-1).count(1, 1)) is not None:
                    pool.wait_ge(s_ht_full, due)
                src = HF[:, :, :].rearrange("p t (o i) -> p t o i", o=1).to_broadcast([P, NT, 2, NI])
                cut(bt, H16[:, 0, :, :, :], H16[:, 1, :, :, :], src, s_h16, 2, 0)

            def attention(bt):
                if not bt.there():
                    return
                pool.wait_ge(s_on, bt.count(3, 3))
                if (due := bt.by(-1).count(1, 1)) is not None:
                    pool.wait_ge(s_wo_full, due)
                cut(bt, OC16[:, 0, :], OC16[:, 1, :], OC[:, :], s_oc16, 2, 0)

            def qk(bt):
                if not bt.there():
                    return
                pool.wait_ge(s_qk, bt.count(2, 2))
                if (due := bt.by(-1).count(2, 2)) is not None:
                    pool.wait_ge(s_selk_full, due)
                if (due := bt.by(-1).count(2, 2)) is not None:
                    pool.wait_ge(s_selq_full, due)
                cut(bt, QK16[:, 0, :, :], QK16[:, 1, :, :], QKF[:, :, :], s_qk16, 2, 0)

            g.memset(HALF[:, :, :], -0.5).then_inc(s_half, 1)
            pool.wait_ge(s_half, 1)
            pool.wait_ge(s_cst, 80)

            def step_all(trip, u):
                i2, i1, i0, m1, m2 = [Batch(trip, u + k) for k in (2, 1, 0, -1, -2)]
                rstd1(i2)
                hidden(m2)
                attention(m1)
                rows1(i2)
                residual(m1)
                rstd2(m1)
                rows2(m1)
                qk(i2)

            run(pool, step_all)


def kernel(L0_attn_hidden_states, L0_attn_Wq, L0_attn_bq, L0_attn_Wk, L0_attn_bk, L0_attn_Wv, L0_attn_bv,
           L0_attn_Wo, L0_attn_bo, L0_attn_dist_emb, L0_ffn_gate_w, L0_ffn_w_gate, L0_ffn_w_up, L0_ffn_w_down):
    import numpy as np
    import concourse.bacc as bacc
    from concourse.bass_utils import run_bass_kernel_spmd

    a = {k: np.asarray(v) for k, v in dict(
        x=L0_attn_hidden_states, wq=L0_attn_Wq, bq=L0_attn_bq, wk=L0_attn_Wk, bk=L0_attn_bk, wv=L0_attn_Wv,
        bv=L0_attn_bv, wo=L0_attn_Wo, bo=L0_attn_bo, dist=L0_attn_dist_emb, gw=L0_ffn_gate_w,
        wg=L0_ffn_w_gate, wu=L0_ffn_w_up, wd=L0_ffn_w_down).items()}

    wo_rows = a["wo"].T.reshape(NG, 4, C, D).transpose(1, 0, 2, 3).reshape(D, D)
    gu = np.stack([a["wg"], a["wu"]], 1).transpose(3, 0, 1, 2).reshape(D, NE * 2 * NI)
    wd = a["wd"].reshape(NE // 2, 2, D, NI).transpose(1, 3, 0, 2).reshape(2 * NI, (NE // 2) * D)
    w_all = np.concatenate([a["wq"].T, a["wk"].T, a["wv"].T, wo_rows, a["gw"].T, gu, wd], axis=1)
    biases = np.stack([a["bq"], a["bk"]], 1)
    b_rows = np.broadcast_to(np.stack([a["bv"], a["bo"]])[None], (P, 2, D))
    at = np.clip(np.arange(TZW)[None, :] - XOFF - np.arange(4)[:, None], -LEFT, RIGHT) + LEFT
    dist_t = np.zeros((4, 4, C, TZW), a["dist"].dtype)
    dist_t[:, 0:3] = a["dist"][at].transpose(0, 2, 1)[:, None]
    dist0 = np.zeros((4, 4, C, 1), a["dist"].dtype)
    dist0[:, 0:3] = a["dist"][0][None, None, :, None]

    sel = np.zeros((NG, 4, C, 4, NG, 4, 4, C), np.float16)
    for g in range(NG):
        for j in range(4):
            for c in range(C):
                for operand, rows in ((0, (0, 1)), (1, (2,)), (2, (0, 2)), (3, (1,))):
                    for row in rows:
                        sel[g, j, c, operand, g, j, row, c] = 1
    kbias = np.zeros((4, 4, C, 1), np.float32)
    kbias[:, 3, 0] = MSCALE
    restrow = np.zeros((4, 4, C, 1), np.float32)
    restrow[:, 1] = -1
    iota = np.broadcast_to(np.arange(NE, dtype=np.float32), (P, NT, NE))
    arrays = {
        "x": a["x"], "w_all": w_all, "biases": biases, "b_rows": b_rows,
        "dist_t": dist_t.reshape(P, TZW), "dist0": dist0.reshape(P, 1),
        "ident16": np.eye(P, dtype=np.float16), "ident32": np.eye(P, dtype=np.float32),
        "sel": sel.reshape(P, 4, NG, P), "kbias": kbias.reshape(P, 1), "restrow": restrow.reshape(P, 1),
        "iota": iota,
    }
    arrays = {k: np.ascontiguousarray(v) for k, v in arrays.items()}

    nc = bacc.Bacc("TRN2", target_bir_lowering=False, num_devices=1)
    args = [nc.dram_tensor(f"in_{k}", v.shape, mybir.dt.from_np(v.dtype), kind="ExternalInput").ap()
            for k, v in arrays.items()]
    out = nc.dram_tensor("out_0", (NB, L, D), F32, kind="ExternalOutput").ap()
    turned_q = nc.dram_tensor("turned_q", (2, 4, P, NG * L // 4), F16, kind="Internal").ap()
    build(nc, *args, turned_q, out)
    r = run_bass_kernel_spmd(nc, [{f"in_{k}": v for k, v in arrays.items()}], core_ids=[0])
    return r.results[0]["out_0"]
```

```python
from contextlib import ExitStack

import concourse.bass as bass
from concourse import mybir

ALU = mybir.AluOpType
ACT = mybir.ActivationFunctionType
F32 = mybir.dt.float32
F16 = mybir.dt.float16
AX_X = mybir.AxisListType.X

P = 128
NB = 16
L = 256
D = 128
NH = 16
C = 8
LEFT, RIGHT = 64, 8
NE = 8
NI = 64
NT = L // P
NG = 4
NCH = 16
QR = 32
NFAR = (P - RIGHT) // QR
NQK = 2 * L + P
SCALE = float(C) ** -0.5
EPS = 1e-5
MSCALE = 64.0
XOFF = L - 4
TZW = XOFF + L
WQ, WK, WV, WO, WG = 0, 128, 256, 384, 512
WGU = WG + NE
WD = WGU + NE * 2 * NI
WALL = WD + (NE // 2) * D


class Batch:

    def __init__(self, trip, off):
        self.trip, self.off = trip, off
        self.par = off % 2
        self.fixed = isinstance(trip, int)

    @property
    def b(self):
        return self.trip * 2 + self.off

    def there(self):
        return not self.fixed or 0 <= self.b < NB

    def by(self, n):
        return Batch(self.trip, self.off + n)

    def count(self, per, k):
        n = self.trip * (2 * per) + (per * self.off + k)
        return None if self.fixed and (n <= 0 or self.b >= NB) else n

    def half(self, per, k):
        return self.trip * per + (per * (self.off // 2) + k) if self.there() else None


def build(nc, x, w_all, biases, edges, b_rows, dist_t, dist0, ident16, ident32, sel, kbias, restrow, iota, turned_q, out):
    with ExitStack() as ctx:
        def sb(name, shape, dt):
            return ctx.enter_context(nc.sbuf_tensor(name, shape, dt))

        def ps(name):
            return ctx.enter_context(nc.psum_tensor(name, [P, 512], F32))

        def sem(name):
            return ctx.enter_context(nc.semaphore(name))

        WF = sb("WF", [P, WALL], F32)
        W16 = sb("W16", [P, 2, WALL], F16)
        BI = sb("BI", [P, 2], F32)
        EDGE = sb("EDGE", [P, 2], F32)
        BFAR = sb("BFAR", [P, 2], F32)
        BR = sb("BR", [P, 2, D], F32)
        TF = sb("TF", [P, TZW], F32)
        TH = sb("TH", [P, TZW], F16)
        TZ = sb("TZ", [P, TZW], F16)
        D0 = sb("D0", [P, 1], F32)
        I16 = sb("I16", [P, P], F16)
        I32 = sb("I32", [P, P], F32)
        SEL = sb("SEL", [P, 4, NG, P], F16)
        KB = sb("KB", [P, 1], F32)
        RESTROW = sb("RESTROW", [P, 1], F32)
        IOTA = sb("IOTA", [P, NT, NE], F32)
        XF = [sb(f"XF{p}", [P, NT, D], F32) for p in range(2)]
        ST1 = sb("ST1", [P, NT, 6], F32)
        MV1 = sb("MV1", [P, NT, 2], F32)
        VE1 = sb("VE1", [P, NT, 1], F32)
        STILL = sb("STILL", [P, 1], F32)
        TABLE = sb("TABLE", [P, NT, 1], F32)
        HALF = sb("HALF", [P, NT, 1], F32)
        RS1 = sb("RS1", [P, NT, 1], F32)
        XNF = sb("XNF", [P, NT, D], F32)
        XN = sb("XN", [P, 2, NT, D], F16)
        XT = sb("XT", [P, 2, L], F16)
        QKF = sb("QKF", [P, NQK], F32)
        QK16 = sb("QK16", [P, 2, NQK], F16)
        QD = sb("QD", [P, NG, L], F16)
        QP = sb("QP", [P, 4, NG, L // 4], F16)
        K4 = [sb(f"K4{p}", [P, NG, L], F16) for p in range(2)]
        KF = [sb(f"KF{p}", [P, NG, P], F16) for p in range(2)]
        Z = [sb(f"Z{p}", [P, 4, NG, L], F16) for p in range(2)]
        R = [sb(f"R{p}", [P, 4, NH, L // 4], F16) for p in range(2)]
        VS = [sb(f"VS{p}", [P, NT, NH, QR], F32) for p in range(2)]
        MXR = sb("MXR", [P, NT, P], F32)
        MXC = sb("MXC", [P, P], F32)
        MN = sb("MN", [P, QR], F32)
        M16 = sb("M16", [P, QR], F16)
        PT = [sb(f"PT{p}", [P, NT, NH, L], F32) for p in range(2)]
        OT = sb("OT", [P, NG, 8, QR], F32)
        RD = sb("RD", [P, NG, 8], F32)
        ON = sb("ON", [P, 8, NG, C], F32)
        OC = sb("OC", [P, L], F32)
        OC16 = sb("OC16", [P, 2, L], F16)
        XB = [sb(f"XB{p}", [P, NT, D], F32) for p in range(2)]
        XBB = sb("XBB", [P, NT, D], F32)
        X2 = [sb(f"X2{p}", [P, NT, D], F32) for p in range(2)]
        ST2 = sb("ST2", [P, NT, 6], F32)
        MV2 = sb("MV2", [P, NT, 2], F32)
        VE2 = sb("VE2", [P, NT, 1], F32)
        RS2 = sb("RS2", [P, NT, 1], F32)
        X2F = sb("X2F", [P, NT, D], F32)
        X2N = sb("X2N", [P, 2, NT, D], F16)
        X2T = sb("X2T", [P, 2, L], F16)
        LMX = sb("LMX", [P, NT], F32)
        LLT = sb("LLT", [P, NT, NE], F32)
        LIX = sb("LIX", [P, NT, NE], F32)
        LID = sb("LID", [P, NT], F16)
        EID = sb("EID", [P, L], F16)
        REX = sb("REX", [P, NT], F32)
        RP1 = sb("RP1", [P, NT], F32)
        RW = sb("RW", [P, NT], F32)
        MK = sb("MK", [P, NE, L], F16)
        XM = sb("XM", [P, 2, NE, L], F16)
        GUF = sb("GUF", [P, NT, 2, NI], F32)
        GE = sb("GE", [P, NT, NI], F32)
        GP = sb("GP", [P, NT, NI], F32)
        GR = sb("GR", [P, NT, NI], F32)
        GS = sb("GS", [P, NT, NI], F32)
        HF = sb("HF", [P, NT, NI], F32)
        H16 = sb("H16", [P, 2, NT, 2, NI], F16)
        HT = sb("HT", [P, 2, L], F16)
        HM = sb("HM", [P, 2, NE // 2, L], F16)
        Y = [sb(f"Y{p}", [P, NT, D], F32) for p in range(2)]

        MX = [ps("MX0"), ps("MX1")]
        SC = [ps("SC0"), ps("SC1")]
        PO = ps("PO")
        BA, BB, BC = ps("BA"), ps("BB"), ps("BC")

        s_cst = sem("s_cst")
        s_wqkvo = sem("s_wqkvo")
        s_wld = sem("s_wld")
        s_zero = sem("s_zero")
        s_ones = sem("s_ones")
        s_w16 = sem("s_w16")
        s_tz = sem("s_tz")
        s_half = sem("s_half")
        s_apart = sem("s_apart")
        s_xf = [sem(f"s_xf{p}") for p in range(2)]
        s_xb = [sem(f"s_xb{p}") for p in range(2)]
        s_r = [sem(f"s_r{p}") for p in range(2)]
        s_qpd = [sem(f"s_qpd{p}") for p in range(2)]
        s_m = [sem(f"s_m{p}") for p in range(2)]
        s_y = [sem(f"s_y{p}") for p in range(2)]
        names = ("still table bfar eid self_full kf z ln1 rs1 xnf xn xt_full xt qk_full qk qk16 selk_full k4 selq_full qd qp v_full v mx_full tr mxc "
                 "mt_full m16 sc_full exp pv_full ot on oc16 xbb wo_full x2 ln2 rs2 x2f x2n x2t_full x2t lg_full "
                 "gate rex eid_full mk xm gu_full guf ge h h16 ht_full ht hm dn_full yf").split()
        S = {n: sem("s_" + n) for n in names}
        (s_still, s_table, s_bfar, s_eid, s_self_full, s_kf, s_z, s_ln1, s_rs1, s_xnf, s_xn, s_xt_full, s_xt, s_qk_full, s_qk, s_qk16, s_selk_full, s_k4, s_selq_full, s_qd,
         s_qp, s_v_full, s_v, s_mx_full, s_tr, s_mxc, s_mt_full, s_m16, s_sc_full, s_exp, s_pv_full,
         s_ot, s_on, s_oc16, s_xbb, s_wo_full, s_x2, s_ln2, s_rs2, s_x2f, s_x2n, s_x2t_full, s_x2t, s_lg_full,
         s_gate, s_rex, s_eid_full, s_mk, s_xm, s_gu_full, s_guf, s_ge, s_h, s_h16, s_ht_full, s_ht,
         s_hm, s_dn_full, s_yf) = [S[n] for n in names]

        def apart(eng, bt):
            if not bt.fixed:
                eng.sem_inc(s_apart, 1)

        def run(eng, step_all):
            for i in range(-2, 4):
                step_all(i // 2, i % 2)
            with eng.Fori(2, 6) as trip:
                for u in range(2):
                    step_all(trip, u)
            for i in range(12, 18):
                step_all(i // 2, i % 2)

        block = ctx.enter_context(nc.Block())

        @block.sync
        def _(sp):
            def load_xf(bt):
                if not bt.there():
                    return
                prev = Batch(bt.trip, bt.off - 2)
                if (due := prev.count(2, 2)) is not None:
                    sp.wait_ge(s_xnf, due)
                apart(sp, bt)
                sp.dma_start(XF[bt.par][:, :, :], x[bass.ds(bt.b, 1), :, :].rearrange(
                    "o (t p) d -> p (o t) d", p=P)).then_inc(s_xf[bt.par], 16)

            def load_xb(bt):
                if not bt.there():
                    return
                if (due := bt.by(-2).count(1, 1)) is not None:
                    sp.wait_ge(s_xbb, due)
                apart(sp, bt)
                sp.dma_start(XB[bt.par][:, :, :], x[bass.ds(bt.b, 1), :, :].rearrange(
                    "o (t p) d -> p (o t) d", p=P)).then_inc(s_xb[bt.par], 16)

            load_xf(Batch(0, 0))
            sp.dma_start(WF[:, 0:WGU], w_all[:, 0:WGU]).then_inc(s_wqkvo, 16)
            for dst, src in ((I16, ident16), (SEL, sel), (KB, kbias), (BI, biases), (EDGE, edges), (BR, b_rows)):
                sp.dma_start(dst[:], src).then_inc(s_cst, 16)
            load_xf(Batch(0, 1))
            for dst, src in ((TF, dist_t), (D0, dist0), (RESTROW, restrow), (I32, ident32), (IOTA, iota)):
                sp.dma_start(dst[:], src).then_inc(s_wld, 16)
            sp.dma_start(WF[:, WGU:WALL], w_all[:, WGU:WALL]).then_inc(s_wld, 16)

            def step_all(trip, u):
                nxt, last, cur, nxt3 = Batch(trip, u + 1), Batch(trip, u - 1), Batch(trip, u), Batch(trip, u + 3)
                if nxt.there():
                    if (due := last.count(NCH, NCH)) is not None:
                        sp.wait_ge(s_sc_full, due)
                        apart(sp, nxt)
                    if nxt.fixed and nxt.b < 2:
                        sp.wait_ge(s_zero, 2 * nxt.b + 2)
                    sp.wait_ge(s_qpd[nxt.par], nxt.half(16, 16))
                    apart(sp, nxt)
                    for a in range(4):
                        sp.dma_start(R[nxt.par][32 * a:32 * a + 32, a, :, :].rearrange(
                            "p (j g) q -> p j (g q)", j=4),
                            turned_q[nxt.par, a].rearrange("(j p) x -> p j x", j=4)).then_inc(s_r[nxt.par], 16)
                if nxt3.there() and not (nxt3.fixed and nxt3.b < 2):
                    load_xf(nxt3)
                if cur.there():
                    load_xb(cur)
                late = Batch(trip, u - 2)
                if late.there():
                    sp.wait_ge(s_yf, late.count(1, 1))
                    apart(sp, late)
                    sp.dma_start(out[bass.ds(late.b, 1), :, :].rearrange("o (t p) d -> p (o t) d", p=P),
                                 Y[late.par][:, :, :]).then_inc(s_y[late.par], 16)
                nxt2 = Batch(trip, u + 2)
                if nxt2.there():
                    if (due := nxt2.by(-2).half(64, 64)) is not None:
                        sp.wait_ge(s_r[nxt2.par], due)
                        apart(sp, nxt2)
                    sp.wait_ge(s_qp, nxt2.count(2, 2))
                    apart(sp, nxt2)
                    sp.dma_start(turned_q[nxt2.par].rearrange("a p x -> p a x"),
                                 QP[:, :, :, :].rearrange("p a g q -> p a (g q)")).then_inc(s_qpd[nxt2.par], 16)
                if nxt.there():
                    sp.wait_ge(s_m16, nxt.count(2, 2))
                    apart(sp, nxt)
                    sp.wait_ge(s_z, nxt.count(4, 4))
                    for j in range(4):
                        row = 32 * j + 3 * C
                        sp.dma_start(Z[nxt.par][row:row + 1, j, :, :].rearrange("o g (b l) -> o (g b) l", l=QR),
                                     M16[32 * j:32 * j + 32, :]).then_inc(s_m[nxt.par], 16)

            run(sp, step_all)
            for par in range(2):
                sp.wait_ge(s_y[par], 16 * NB // 2)

        @block.tensor
        def _(pe):
            mm = nc.tensor.matmul

            def three(out_ap, stat, mov, start, stop):
                mm(out_ap, stat(0), mov(0), start=start, stop=False, skip_group_check=True)
                mm(out_ap, stat(0), mov(1), start=False, stop=False, skip_group_check=True)
                return mm(out_ap, stat(1), mov(0), start=False, stop=stop, skip_group_check=True)

            def chunk(bank, bt, n):
                lb, rt = n // 2, n % 2
                groups = [q for q in range(8 * lb, 8 * lb + 8)
                          if not (rt + 1) * P - 1 <= 4 * q - LEFT]
                far = rt == 1 and lb < NFAR
                if far:
                    groups = []
                for g in range(NG):
                    last = mm(bank[:, P * g:P * g + P], KF[bt.par][:, g, :] if far else K4[bt.par][:, g, P * rt:P * rt + P],
                              Z[bt.par][:, :, g, QR * lb:QR * lb + QR],
                              start=g == 0, stop=g == NG - 1 and not groups, skip_group_check=True)
                outs = bank[:, :].rearrange("p (g j q a) -> p g j q a", g=NG, j=4, a=4)
                rel = R[bt.par][:, :, :, :].rearrange("p a (j g) q -> p g j a q", j=4)
                for q in groups:
                    at = XOFF + P * rt - 4 * q
                    last = mm(outs[:, :, :, q - 8 * lb, :], TZ[:, at:at + P], rel[:, :, :, :, q],
                              start=False, stop=q == groups[-1], skip_group_check=True)
                return last

            def max_chunk(bt, n):
                if not bt.there():
                    return
                if n == 0:
                    pe.wait_ge(s_z, bt.count(4, 4))
                    pe.wait_ge(s_r[bt.par], bt.half(64, 64))
                    pe.wait_ge(s_k4, bt.count(2, 2))
                    pe.wait_ge(s_kf, bt.count(1, 1))
                    if bt.fixed and bt.b == 0:
                        pe.wait_ge(s_tz, 3)
                if (due := bt.count(NCH, n - 1)) is not None:
                    pe.wait_ge(s_tr, due)
                chunk(MX[n % 2], bt, n).then_inc(s_mx_full, 1)

            def score_chunk(bt, n):
                if not bt.there():
                    return
                if n == 0:
                    pe.wait_ge(s_m[bt.par], bt.half(64, 64))
                if (due := bt.count(NCH, n - 1)) is not None:
                    pe.wait_ge(s_exp, due)
                chunk(SC[n % 2], bt, n).then_inc(s_sc_full, 1)

            def select(bank, kind, tokens, groups, full):
                wide = tokens.stop - tokens.start
                for n, g in enumerate(groups):
                    o = bank[:, wide * n:wide * n + wide]
                    mm(o, SEL[:, 2 * kind, g, :], QK16[:, 0, tokens], start=True, stop=False)
                    last = mm(o, SEL[:, 2 * kind + 1, g, :], QK16[:, 1, tokens], start=False, stop=True)
                last.then_inc(full, 1)

            def keys_far(bt):
                if not bt.there():
                    return
                pe.wait_ge(s_qk16, bt.count(2, 2))
                if (due := bt.by(-3).count(1, 1)) is not None:
                    pe.wait_ge(s_eid, due)
                if (due := bt.by(-1).count(1, 1)) is not None:
                    pe.wait_ge(s_kf, due)
                select(BB, 1, slice(2 * L, NQK), range(NG), s_self_full)

            def keys(bt):
                if not bt.there():
                    return
                pe.wait_ge(s_qk16, bt.count(2, 2))
                pe.wait_ge(s_qd, bt.count(2, 2))
                if (due := bt.by(-1).count(2, 1)) is not None:
                    pe.wait_ge(s_m16, due)
                select(BA, 1, slice(L, 2 * L), (0, 1), s_selk_full)
                select(BC, 1, slice(L, 2 * L), (2, 3), s_selk_full)

            def pv(bt, half):
                if not bt.there():
                    return
                if half == 0:
                    pe.wait_ge(s_v, bt.count(1, 1))
                    pe.wait_ge(s_exp, bt.count(NCH, NCH))
                if (due := bt.count(2, half)) is not None:
                    pe.wait_ge(s_ot, due)
                for gg in range(2):
                    for rt in range(NT):
                        for j in range(4):
                            h = 4 * (2 * half + gg) + j
                            last = mm(PO[32 * j:32 * j + 32, L * gg:L * gg + L], VS[bt.par][:, rt, h, :],
                                      PT[bt.par][:, rt, h, :], start=rt == 0, stop=rt == NT - 1,
                                      skip_group_check=True)
                last.then_inc(s_pv_full, 1)

            def values(bt):
                if not bt.there():
                    return
                pe.wait_ge(s_k4, bt.count(2, 2))
                for t in range(NT):
                    last = three(BC[:, D * t:D * t + D], lambda s: XT[:, s, P * t:P * t + P],
                                 lambda s: W16[:, s, WV:WV + D], True, True)
                last.then_inc(s_v_full, 1)

            def turn(bank, src, full):
                o = bank[:, 0:2 * P].bitcast(F16)
                for s in range(2):
                    for t in range(NT):
                        c = (s * NT + t) * P
                        last = nc.tensor.transpose(o[:, c:c + P], src(s, t), I16[:, :])
                last.then_inc(full, 1)

            def h_turn(bt):
                if not bt.there():
                    return
                pe.wait_ge(s_h16, bt.count(2, 2))
                pe.wait_ge(s_eid, bt.count(1, 1))
                if (due := bt.by(1).count(1, 1)) is not None:
                    pe.wait_ge(s_x2, due)
                turn(BB, lambda s, t: H16[:, s, t, :, :].rearrange("p a i -> p (a i)"), s_ht_full)

            def x_turn(bt):
                if not bt.there():
                    return
                pe.wait_ge(s_xn, bt.count(2, 2))
                if (due := bt.by(-1).count(2, 1)) is not None:
                    pe.wait_ge(s_k4, due)
                if (due := bt.by(-4).count(1, 1)) is not None:
                    pe.wait_ge(s_guf, due)
                turn(BA, lambda s, t: XN[:, s, t, :], s_xt_full)

            def project_out(bt):
                if not bt.there():
                    return
                pe.wait_ge(s_oc16, bt.count(2, 2))
                if (due := bt.by(-1).count(1, 1)) is not None:
                    pe.wait_ge(s_eid, due)
                if (due := bt.by(2).count(1, 1)) is not None:
                    pe.wait_ge(s_kf, due)
                for t in range(NT):
                    last = three(BB[:, D * t:D * t + D], lambda s: OC16[:, s, P * t:P * t + P],
                                 lambda s: W16[:, s, WO:WO + D], True, True)
                last.then_inc(s_wo_full, 1)

            def project_qk(bt):
                if not bt.there():
                    return
                if bt.fixed and bt.b == 0:
                    pe.wait_ge(s_w16, 2)
                pe.wait_ge(s_xt, bt.count(1, 1))
                for kind, w in enumerate((WQ, WK)):
                    last = three(BA[:, L * kind:L * kind + L], lambda s: W16[:, s, w:w + D],
                                 lambda s: XT[:, s, :], True, True)
                last.then_inc(s_qk_full, 1)

            def down(bt):
                if not bt.there():
                    return
                pe.wait_ge(s_hm, bt.count(2, 2))
                for t in range(NT):
                    for e in range(NE // 2):
                        last = three(BB[:, D * t:D * t + D], lambda s: HM[:, s, e, P * t:P * t + P],
                                     lambda s: W16[:, s, WD + D * e:WD + D * e + D], e == 0, e == NE // 2 - 1)
                last.then_inc(s_dn_full, 1)

            def x2_turn(bt):
                if not bt.there():
                    return
                pe.wait_ge(s_x2n, bt.count(2, 2))
                if (due := bt.by(2).count(1, 1)) is not None:
                    pe.wait_ge(s_v, due)
                turn(BC, lambda s, t: X2N[:, s, t, :], s_x2t_full)

            def queries(bt, half):
                if not bt.there():
                    return
                if half == 0:
                    pe.wait_ge(s_qk16, bt.count(2, 2))
                    select(BA, 0, slice(0, L), (0, 1), s_selq_full)
                else:
                    if (due := bt.by(-1).count(1, 1)) is not None:
                        pe.wait_ge(s_v, due)
                    if (due := bt.by(-3).count(1, 1)) is not None:
                        pe.wait_ge(s_x2t, due)
                    select(BC, 0, slice(0, L), (2, 3), s_selq_full)

            def logits(bt):
                if not bt.there():
                    return
                pe.wait_ge(s_x2t, bt.count(1, 1))
                if (due := bt.by(-1).count(1, 1)) is not None:
                    pe.wait_ge(s_yf, due)
                for t in range(NT):
                    last = three(BB[:, NE * t:NE * t + NE], lambda s: X2T[:, s, P * t:P * t + P],
                                 lambda s: W16[:, s, WG:WG + NE], True, True)
                last.then_inc(s_lg_full, 1)

            def max_turn(bt):
                if not bt.there():
                    return
                if bt.fixed and bt.b == 0:
                    pe.wait_ge(s_wld, 96)
                pe.wait_ge(s_mxc, bt.count(1, 1))
                if (due := bt.by(1).count(2, 1)) is not None:
                    pe.wait_ge(s_qd, due)
                nc.tensor.transpose(BA[:, 0:P], MXC[:, :], I32[:, :]).then_inc(s_mt_full, 1)

            def experts(bt):
                if not bt.there():
                    return
                pe.wait_ge(s_gate, bt.count(6, 4))
                for t in range(NT):
                    last = mm(BB[:, P * t:P * t + P], LID[:, t:t + 1].to_broadcast([P, P]), I16[:, :],
                              start=True, stop=True)
                last.then_inc(s_eid_full, 1)

            def gate_up(bt):
                if not bt.there():
                    return
                if bt.fixed and bt.b == 0:
                    pe.wait_ge(s_w16, 4)
                pe.wait_ge(s_xm, bt.count(2, 2))
                if (due := bt.by(2).count(2, 1)) is not None:
                    pe.wait_ge(s_m16, due)
                if (due := bt.by(3).count(2, 1)) is not None:
                    pe.wait_ge(s_k4, due)
                for t in range(NT):
                    for e in range(NE):
                        last = three(BA[:, D * t:D * t + D], lambda s: XM[:, s, e, P * t:P * t + P],
                                     lambda s: W16[:, s, WGU + 2 * NI * e:WGU + 2 * NI * (e + 1)],
                                     e == 0, e == NE - 1)
                last.then_inc(s_gu_full, 1)

            pe.wait_ge(s_cst, 96)

            def step_all(trip, u):
                i2, i1, i0, m1, m2 = [Batch(trip, u + k) for k in (2, 1, 0, -1, -2)]
                score_chunk(m1, 14)
                max_chunk(i0, 14)
                max_chunk(i0, 15)
                experts(m2)
                score_chunk(m1, 15)
                queries(i1, 1)
                keys_far(i1)
                max_turn(i0)
                pv(m1, 0)
                keys(i1)
                pv(m1, 1)
                gate_up(m2)
                max_chunk(i1, 0)
                max_chunk(i1, 1)
                score_chunk(i0, 0)
                score_chunk(i0, 1)
                max_chunk(i1, 2)
                x_turn(i2)
                score_chunk(i0, 2)
                score_chunk(i0, 3)
                max_chunk(i1, 3)
                values(i1)
                project_out(m1)
                score_chunk(i0, 4)
                max_chunk(i1, 4)
                score_chunk(i0, 5)
                max_chunk(i1, 5)
                score_chunk(i0, 6)
                project_qk(i2)
                h_turn(m2)
                max_chunk(i1, 6)
                score_chunk(i0, 7)
                max_chunk(i1, 7)
                score_chunk(i0, 8)
                max_chunk(i1, 8)
                max_chunk(i1, 9)
                score_chunk(i0, 9)
                max_chunk(i1, 10)
                score_chunk(i0, 10)
                max_chunk(i1, 11)
                x2_turn(m1)
                score_chunk(i0, 11)
                score_chunk(i0, 12)
                down(m2)
                max_chunk(i1, 12)
                max_chunk(i1, 13)
                queries(i2, 0)
                logits(m1)
                score_chunk(i0, 13)

            run(pe, step_all)

        @block.scalar
        def _(act):
            copy = nc.scalar.activation

            def exps(bt, n):
                if not bt.there():
                    return
                lb, rt = n // 2, n % 2
                if n == 0:
                    if (due := bt.by(-2).count(2, 2)) is not None:
                        act.wait_ge(s_pv_full, due)
                act.wait_ge(s_sc_full, bt.count(NCH, n + 1))
                copy(PT[bt.par][:, rt, :, QR * lb:QR * lb + QR],
                     SC[n % 2][:, :].rearrange("p (h l) -> p h l", h=NH), ACT.Exp,
                     scale=SCALE).then_inc(s_exp, 1)

            def keys(bt):
                if not bt.there():
                    return
                if (due := bt.by(-2).count(NCH, NCH)) is not None:
                    act.wait_ge(s_sc_full, due)
                for half, bank in enumerate((BA, BC)):
                    act.wait_ge(s_selk_full, bt.count(2, half + 1))
                    copy(K4[bt.par][:, 2 * half:2 * half + 2, :],
                         bank[:, :].rearrange("p (g l) -> p g l", g=2), ACT.Identity,
                         bias=KB[:, 0:1]).then_inc(s_k4, 1)

            def keys_far(bt):
                if not bt.there():
                    return
                if (due := bt.by(-2).count(NCH, NCH)) is not None:
                    act.wait_ge(s_sc_full, due)
                act.wait_ge(s_self_full, bt.count(1, 1))
                copy(KF[bt.par][:, :, :], BB[:, :].rearrange("p (g l) -> p g l", g=NG), ACT.Identity,
                     bias=KB[:, 0:1]).then_inc(s_kf, 1)

            def queries(bt, half):
                if not bt.there():
                    return
                if half == 0:
                    if (due := bt.by(-1).count(4, 4)) is not None:
                        act.wait_ge(s_z, due)
                    if (due := bt.by(-1).half(16, 16)) is not None:
                        act.wait_ge(s_qpd[1 - bt.par], due)
                act.wait_ge(s_selq_full, bt.count(2, half + 1))
                copy(QP[:, :, 2 * half:2 * half + 2, :],
                     (BA, BC)[half][:, :].rearrange("p (g q a) -> p a g q", g=2, a=4),
                     ACT.Copy).then_inc(s_qp, 1)
                copy(QD[:, 2 * half:2 * half + 2, :],
                     (BA, BC)[half][:, :].rearrange("p (g l) -> p g l", g=2),
                     ACT.Copy).then_inc(s_qd, 1)

            def turned(bank):
                return bank[:, 0:2 * P].bitcast(F16).rearrange("p (s l) -> p s l", s=2)

            def turned_x1(bt):
                if not bt.there():
                    return
                if (due := bt.by(-1).count(1, 1)) is not None:
                    act.wait_ge(s_v_full, due)
                act.wait_ge(s_xt_full, bt.count(1, 1))
                copy(XT[:, :, :], turned(BA), ACT.Copy).then_inc(s_xt, 1)

            def turned_x2(bt):
                if not bt.there():
                    return
                if (due := bt.by(-1).count(2, 2)) is not None:
                    act.wait_ge(s_xm, due)
                act.wait_ge(s_x2t_full, bt.count(1, 1))
                copy(X2T[:, :, :], turned(BC), ACT.Copy).then_inc(s_x2t, 1)

            def turned_h(bt):
                if not bt.there():
                    return
                if (due := bt.by(-1).count(2, 2)) is not None:
                    act.wait_ge(s_hm, due)
                act.wait_ge(s_ht_full, bt.count(1, 1))
                copy(HT[:, :, :], turned(BB), ACT.Copy).then_inc(s_ht, 1)

            def qk(bt):
                if not bt.there():
                    return
                if (due := bt.by(-1).count(2, 2)) is not None:
                    act.wait_ge(s_qk16, due)
                act.wait_ge(s_qk_full, bt.count(1, 1))
                for kind in range(2):
                    copy(QKF[:, L * kind:L * kind + L], BA[:, L * kind:L * kind + L], ACT.Identity,
                         bias=BI[:, kind:kind + 1]).then_inc(s_qk, 1)
                if bt.fixed and bt.b == 0:
                    act.wait_ge(s_bfar, 2)
                copy(QKF[:, 2 * L:NQK], BA[:, L + P:2 * L], ACT.Identity, bias=BFAR[:, 1:2]).then_inc(s_qk, 1)

            def experts(bt):
                if not bt.there():
                    return
                if (due := bt.by(-1).count(NE, NE)) is not None:
                    act.wait_ge(s_mk, due)
                act.wait_ge(s_eid_full, bt.count(1, 1))
                copy(EID[:, :], BB[:, 0:L], ACT.Copy).then_inc(s_eid, 1)

            def rw_exp(bt):
                if not bt.there():
                    return
                if (due := bt.by(-1).count(6, 5)) is not None:
                    act.wait_ge(s_gate, due)
                act.wait_ge(s_gate, bt.count(6, 1))
                copy(REX[:, :], LMX[:, :], ACT.Exp, scale=-1.0).then_inc(s_rex, 1)

            def gate_exp(bt):
                if not bt.there():
                    return
                if (due := bt.by(-1).count(4, 1)) is not None:
                    act.wait_ge(s_h, due)
                act.wait_ge(s_guf, bt.count(1, 1))
                copy(GE[:, :, :], GUF[:, :, 0, :], ACT.Exp, scale=-1.0).then_inc(s_ge, 1)

            act.wait_ge(s_half, 1)
            copy(TABLE[:, :, :], HALF[:, :, :], ACT.Exp).then_inc(s_table, 1)
            act.wait_ge(s_cst, 96)

            def step_all(trip, u):
                i2, i1, i0, m1, m2 = [Batch(trip, u + k) for k in (2, 1, 0, -1, -2)]
                exps(m1, 10)
                turned_x2(m2)
                exps(m1, 11)
                exps(m1, 12)
                queries(i1, 0)
                exps(m1, 13)
                rw_exp(m2)
                exps(m1, 14)
                experts(m2)
                exps(m1, 15)
                queries(i1, 1)
                keys(i1)
                keys_far(i1)
                gate_exp(m2)
                exps(i0, 0)
                exps(i0, 1)
                exps(i0, 2)
                exps(i0, 3)
                turned_x1(i2)
                exps(i0, 4)
                exps(i0, 5)
                exps(i0, 6)
                turned_h(m2)
                qk(i2)
                exps(i0, 7)
                exps(i0, 8)
                exps(i0, 9)

            run(act, step_all)

        @block.vector
        def _(dve):
            v = nc.vector

            def stats(bt, src, st, mv, done, ready, used):
                ready()
                for t in range(NT):
                    v.bn_stats(st[:, t, :], src[:, t, :]).then_inc(done, 1)
                used()
                for t in range(NT):
                    dve.wait_ge(done, bt.count(4, t + 1))
                    apart(dve, bt)
                    v.bn_aggr(mv[:, t, :], st[:, t, :]).then_inc(done, 1)

            def ln1(bt):
                if not bt.there():
                    return
                before = Batch(bt.trip, bt.off - 1)

                def used():
                    if (due := before.count(2, 2)) is not None:
                        dve.wait_ge(s_xnf, due)

                def ready():
                    if (due := before.count(4, 4)) is not None:
                        dve.wait_ge(s_ln1, due)
                    dve.wait_ge(s_xf[bt.par], bt.half(16, 16))
                stats(bt, XF[bt.par], ST1, MV1, s_ln1, ready, used)

            def normalise(bt, src, mv, rs, full, done):
                for t in range(NT):
                    v.tensor_scalar(full[:, t, :], src[:, t, :], mv[:, t, 0:1], rs[:, t, :],
                                    ALU.subtract, ALU.mult).then_inc(done, 1)

            def far_bias():
                dve.wait_ge(s_cst, 96)
                v.tensor_tensor(BFAR[:, 0:1], EDGE[:, 0:1], EDGE[:, 1:2], ALU.subtract).then_inc(s_bfar, 1)
                dve.wait_ge(s_bfar, 1)
                v.tensor_tensor(BFAR[:, 1:2], BFAR[:, 0:1], BI[:, 1:2], ALU.add).then_inc(s_bfar, 1)

            def cut_projections():
                dve.wait_ge(s_wqkvo, 16)
                v.tensor_copy(W16[:, 0, 0:WGU], WF[:, 0:WGU]).then_inc(s_w16, 1)
                dve.wait_ge(s_w16, 1)
                v.tensor_tensor(W16[:, 1, 0:WGU], WF[:, 0:WGU], W16[:, 0, 0:WGU], ALU.subtract).then_inc(s_w16, 1)

            def other_constants():
                v.memset(R[0][:], 0.0).then_inc(s_zero, 1)
                dve.wait_ge(s_wld, 96)
                v.tensor_scalar(TF[:, :], TF[:, :], D0[:, 0:1], None, ALU.subtract).then_inc(s_tz, 1)
                dve.wait_ge(s_tz, 1)
                v.tensor_copy(TH[:, :], TF[:, :]).then_inc(s_tz, 1)
                dve.wait_ge(s_tz, 2)
                v.scalar_tensor_tensor(TZ[:, :], TH[:, :], RESTROW[:, 0:1], TF[:, :],
                                       ALU.mult, ALU.add).then_inc(s_tz, 1)
                v.memset(Z[1][:], 0.0).then_inc(s_zero, 1)
                v.memset(R[1][:], 0.0).then_inc(s_zero, 1)
                v.tensor_copy(W16[:, 0, WGU:WALL], WF[:, WGU:WALL]).then_inc(s_w16, 1)
                dve.wait_ge(s_w16, 3)
                v.tensor_tensor(W16[:, 1, WGU:WALL], WF[:, WGU:WALL], W16[:, 0, WGU:WALL],
                                ALU.subtract).then_inc(s_w16, 1)

            def norm1(bt):
                if not bt.there():
                    return
                if bt.fixed and bt.b == 0:
                    cut_projections()
                dve.wait_ge(s_rs1, bt.count(2, 2))
                if (due := bt.by(-1).count(2, 2)) is not None:
                    dve.wait_ge(s_xn, due)
                apart(dve, bt)
                normalise(bt, XF[bt.par], MV1, RS1, XNF, s_xnf)
                if bt.fixed and bt.b == 0:
                    far_bias()
                    other_constants()

            def norm2(bt):
                if not bt.there():
                    return
                dve.wait_ge(s_rs2, bt.count(2, 2))
                if (due := bt.by(-1).count(2, 2)) is not None:
                    dve.wait_ge(s_x2n, due)
                apart(dve, bt)
                normalise(bt, X2[bt.par], MV2, RS2, X2F, s_x2f)

            def gates_scale(bt):
                if not bt.there():
                    return
                dve.wait_ge(s_gu_full, bt.count(1, 1))
                dve.wait_ge(s_gate, bt.count(6, 6))
                if (due := bt.by(-1).count(1, 1)) is not None:
                    dve.wait_ge(s_ge, due)
                if (due := bt.by(-1).count(4, 4)) is not None:
                    dve.wait_ge(s_h, due)
                v.tensor_tensor(GUF[:, :, :, :].rearrange("p t a i -> p t (a i)"),
                                BA[:, 0:NT * D].rearrange("p (t d) -> p t d", t=NT),
                                RW[:, :].rearrange("p (t o) -> p t o", o=1).to_broadcast([P, NT, D]),
                                ALU.mult).then_inc(s_guf, 1)

            def hidden(bt):
                if not bt.there():
                    return
                dve.wait_ge(s_ge, bt.count(1, 1))
                v.tensor_scalar(GP[:, :, :], GE[:, :, :], 1.0, None, ALU.add).then_inc(s_h, 1)
                dve.wait_ge(s_h, bt.count(4, 1))
                v.reciprocal(GR[:, :, :], GP[:, :, :]).then_inc(s_h, 1)
                dve.wait_ge(s_h, bt.count(4, 2))
                v.tensor_tensor(GS[:, :, :], GUF[:, :, 0, :], GR[:, :, :], ALU.mult).then_inc(s_h, 1)
                dve.wait_ge(s_h, bt.count(4, 3))
                if (due := bt.by(-1).count(2, 2)) is not None:
                    dve.wait_ge(s_h16, due)
                v.tensor_tensor(HF[:, :, :], GS[:, :, :], GUF[:, :, 1, :], ALU.mult).then_inc(s_h, 1)

            def out_turn(bt, half):
                if not bt.there():
                    return
                if half == 0:
                    if (due := bt.by(-1).count(3, 2)) is not None:
                        dve.wait_ge(s_on, due)
                dve.wait_ge(s_pv_full, bt.count(2, half + 1))
                v.transpose(OT[:, 2 * half:2 * half + 2, :, :].rearrange("p g b r -> p (g b r)"),
                            PO[:, :]).then_inc(s_ot, 1)

            def out_norm(bt):
                if not bt.there():
                    return
                dve.wait_ge(s_ot, bt.count(2, 2))
                v.reciprocal(RD[:, :, :], OT[:, :, :, C]).then_inc(s_on, 1)
                dve.wait_ge(s_on, bt.count(3, 1))
                v.tensor_tensor(ON[:, :, :, :].rearrange("p b g c -> p g b c"), OT[:, :, :, 0:C],
                                RD[:, :, :].rearrange("p g (b o) -> p g b o", o=1).to_broadcast([P, NG, 8, C]),
                                ALU.mult).then_inc(s_on, 1)
                dve.wait_ge(s_on, bt.count(3, 2))
                if (due := bt.by(-1).count(2, 2)) is not None:
                    dve.wait_ge(s_oc16, due)
                v.transpose(OC[:, :], ON[:, :, :, :].rearrange("p b g c -> p (b g c)")).then_inc(s_on, 1)

            def values(bt):
                if not bt.there():
                    return
                if bt.fixed and bt.b < 2:
                    dve.wait_ge(s_ones, 2)
                    dve.wait_ge(s_cst, 96)
                dve.wait_ge(s_v_full, bt.count(1, 1))
                if (due := bt.by(-2).count(2, 2)) is not None:
                    dve.wait_ge(s_pv_full, due)
                v.tensor_tensor(VS[bt.par][:, :, :, 0:C],
                                BC[:, 0:NT * D].rearrange("p (t h c) -> p t h c", t=NT, c=C),
                                BR[:, 0:1, :].rearrange("p o (h c) -> p o h c", c=C)
                                .to_broadcast([P, NT, NH, C]), ALU.add).then_inc(s_v, 1)

            def maxima(bt, n):
                if not bt.there():
                    return
                lb, rt = n // 2, n % 2
                if n == 0:
                    if (due := bt.by(-1).count(1, 1)) is not None:
                        dve.wait_ge(s_mxc, due)
                dve.wait_ge(s_mx_full, bt.count(NCH, n + 1))
                v.tensor_reduce(
                    MXR[:, rt, :].rearrange("p (j g b) -> p g j b", j=4, b=8)[:, :, :, lb],
                    MX[n % 2][:, :].rearrange("p (h l) -> p h l", l=QR), axis=AX_X, op=ALU.max,
                    apply_transpose=True).then_inc(s_tr, 1)

            def hidden_mask(bt):
                if not bt.there():
                    return
                dve.wait_ge(s_ht, bt.count(1, 1))
                dve.wait_ge(s_mk, bt.count(NE, NE))
                if (due := bt.by(-1).count(1, 1)) is not None:
                    dve.wait_ge(s_dn_full, due)
                for e2 in range(2):
                    q = slice(NI * e2, NI * e2 + NI)
                    mk = MK[q, :, :].rearrange("p (e two) l -> p e two l", two=2)[:, :, e2, :]
                    for s in range(2):
                        last = v.tensor_tensor(HM[q, s, :, :],
                                               HT[q, s:s + 1, :].to_broadcast([NI, NE // 2, L]),
                                               mk, ALU.mult)
                    last.then_inc(s_hm, 1)

            def attended(bt):
                if not bt.there():
                    return
                dve.wait_ge(s_wo_full, bt.count(1, 1))
                dve.wait_ge(s_xbb, bt.count(1, 1))
                if (due := bt.by(-2).count(1, 1)) is not None:
                    dve.wait_ge(s_yf, due)
                v.tensor_tensor(X2[bt.par][:, :, :], BB[:, 0:NT * D].rearrange("p (t d) -> p t d", t=NT),
                                XBB[:, :, :], ALU.add).then_inc(s_x2, 1)
                before = Batch(bt.trip, bt.off - 1)

                def ready():
                    dve.wait_ge(s_x2, bt.count(1, 1))
                    if (due := before.count(4, 4)) is not None:
                        dve.wait_ge(s_ln2, due)

                def used():
                    if (due := before.count(2, 2)) is not None:
                        dve.wait_ge(s_x2f, due)
                stats(bt, X2[bt.par], ST2, MV2, s_ln2, ready, used)

            def result(bt):
                if not bt.there():
                    return
                dve.wait_ge(s_dn_full, bt.count(1, 1))
                prev = Batch(bt.trip, bt.off - 2)
                if (due := prev.half(16, 16)) is not None:
                    dve.wait_ge(s_y[prev.par], due)
                v.tensor_tensor(Y[bt.par][:, :, :], BB[:, 0:NT * D].rearrange("p (t d) -> p t d", t=NT),
                                X2[bt.par][:, :, :], ALU.add).then_inc(s_yf, 1)

            def gate(bt):
                if not bt.there():
                    return
                before = Batch(bt.trip, bt.off - 1)
                lg = BB[:, 0:NT * NE].rearrange("p (t e) -> p t e", t=NT)
                dve.wait_ge(s_lg_full, bt.count(1, 1))
                if (due := before.count(1, 1)) is not None:
                    dve.wait_ge(s_rex, due)
                v.tensor_reduce(LMX[:, :], lg, axis=AX_X, op=ALU.max).then_inc(s_gate, 1)
                dve.wait_ge(s_gate, bt.count(6, 1))
                v.tensor_tensor(LLT[:, :, :], lg,
                                LMX[:, :].rearrange("p (t o) -> p t o", o=1).to_broadcast([P, NT, NE]),
                                ALU.is_lt).then_inc(s_gate, 1)
                dve.wait_ge(s_gate, bt.count(6, 2))
                v.scalar_tensor_tensor(LIX[:, :, :], LLT[:, :, :], float(NE), IOTA[:, :, :],
                                       ALU.mult, ALU.add).then_inc(s_gate, 1)
                dve.wait_ge(s_gate, bt.count(6, 3))
                if (due := before.count(1, 1)) is not None:
                    dve.wait_ge(s_eid_full, due)
                v.tensor_reduce(LID[:, :], LIX[:, :, :], axis=AX_X, op=ALU.min).then_inc(s_gate, 1)

            def weight(bt):
                if not bt.there():
                    return
                before = Batch(bt.trip, bt.off - 1)
                dve.wait_ge(s_rex, bt.count(1, 1))
                v.tensor_scalar(RP1[:, :], REX[:, :], 1.0, None, ALU.add).then_inc(s_gate, 1)
                dve.wait_ge(s_gate, bt.count(6, 5))
                if (due := before.count(1, 1)) is not None:
                    dve.wait_ge(s_guf, due)
                v.reciprocal(RW[:, :], RP1[:, :]).then_inc(s_gate, 1)

            def max_join(bt):
                if not bt.there():
                    return
                dve.wait_ge(s_tr, bt.count(NCH, NCH))
                if (due := bt.by(-1).count(1, 1)) is not None:
                    dve.wait_ge(s_mt_full, due)
                v.tensor_tensor(MXC[:, :], MXR[:, 0, :], MXR[:, 1, :], ALU.max).then_inc(s_mxc, 1)

            def max_cut(bt):
                if not bt.there():
                    return
                dve.wait_ge(s_mt_full, bt.count(1, 1))
                if (due := bt.by(-1).count(2, 2)) is not None:
                    dve.wait_ge(s_m16, due)
                v.tensor_reduce(MN[:, :], BA[:, 0:P].rearrange("p (q l) -> p l q", q=4), axis=AX_X,
                                op=ALU.max).then_inc(s_m16, 1)
                dve.wait_ge(s_m16, bt.count(2, 1))
                if (due := bt.by(-1).half(64, 64)) is not None:
                    dve.wait_ge(s_m[1 - bt.par], due)
                v.tensor_scalar(M16[:, :], MN[:, :], -1.0 / MSCALE, None, ALU.mult).then_inc(s_m16, 1)

            def masks(bt):
                if not bt.there():
                    return
                dve.wait_ge(s_eid, bt.count(1, 1))
                if (due := bt.by(-1).count(2, 2)) is not None:
                    dve.wait_ge(s_hm, due)
                if (due := bt.by(-1).count(2, 2)) is not None:
                    dve.wait_ge(s_xm, due)
                for e in range(NE):
                    v.tensor_scalar(MK[:, e, :], EID[:, :], float(e), None, ALU.is_equal).then_inc(s_mk, 1)

            def rows_mask(bt, half):
                if not bt.there():
                    return
                if half == 0:
                    if (due := bt.by(-1).count(1, 1)) is not None:
                        dve.wait_ge(s_gu_full, due)
                dve.wait_ge(s_x2t, bt.count(1, 1))
                dve.wait_ge(s_mk, bt.count(NE, 4 * half + 4))
                e = slice(4 * half, 4 * half + 4)
                for s in range(2):
                    last = v.tensor_tensor(XM[:, s, e, :], X2T[:, s:s + 1, :].to_broadcast([P, 4, L]),
                                           MK[:, e, :], ALU.mult)
                last.then_inc(s_xm, 1)

            v.memset(Z[0][:], 0.0).then_inc(s_zero, 1)

            def step_all(trip, u):
                i2, i1, i0, m1, m2 = [Batch(trip, u + k) for k in (2, 1, 0, -1, -2)]
                rows_mask(m2, 0)
                out_turn(m1, 0)
                rows_mask(m2, 1)
                weight(m2)
                ln1(i2)
                out_turn(m1, 1)
                norm1(i2)
                out_norm(m1)
                gates_scale(m2)
                maxima(i1, 0)
                maxima(i1, 1)
                hidden(m2)
                maxima(i1, 2)
                maxima(i1, 3)
                attended(m1)
                maxima(i1, 4)
                maxima(i1, 5)
                norm2(m1)
                maxima(i1, 6)
                maxima(i1, 7)
                values(i1)
                maxima(i1, 8)
                maxima(i1, 9)
                hidden_mask(m2)
                maxima(i1, 10)
                maxima(i1, 11)
                result(m2)
                maxima(i1, 12)
                maxima(i1, 13)
                gate(m1)
                maxima(i1, 14)
                maxima(i1, 15)
                max_join(i1)
                masks(m1)
                max_cut(i1)

            run(dve, step_all)

        @block.gpsimd
        def _(pool):
            g = nc.gpsimd

            def cut(bt, hi, lo, src, done, per, k):
                apart(pool, bt)
                g.tensor_scalar(hi, src, 1.0, 0.0, ALU.mult, ALU.add).then_inc(done, 1)
                pool.wait_ge(done, bt.count(per, k + 1))
                g.tensor_tensor(lo, src, hi, ALU.subtract).then_inc(done, 1)

            def rstd1(bt):
                if not bt.there():
                    return
                if (due := bt.by(-1).count(2, 2)) is not None:
                    pool.wait_ge(s_rs1, due)
                pool.wait_ge(s_ln1, bt.count(4, 4))
                apart(pool, bt)
                g.tensor_scalar(VE1[:, :, :], MV1[:, :, 1:2], EPS, None, ALU.add).then_inc(s_rs1, 1)
                pool.wait_ge(s_rs1, bt.count(2, 1))
                g.tensor_tensor(RS1[:, :, :], VE1[:, :, :], HALF[:, :, :], ALU.pow).then_inc(s_rs1, 1)

            def rstd2(bt):
                if not bt.there():
                    return
                if (due := bt.by(-1).count(2, 2)) is not None:
                    pool.wait_ge(s_rs2, due)
                pool.wait_ge(s_ln2, bt.count(4, 4))
                apart(pool, bt)
                g.tensor_scalar(VE2[:, :, :], MV2[:, :, 1:2], EPS, None, ALU.add).then_inc(s_rs2, 1)
                pool.wait_ge(s_rs2, bt.count(2, 1))
                g.tensor_tensor(RS2[:, :, :], VE2[:, :, :], HALF[:, :, :], ALU.pow).then_inc(s_rs2, 1)

            def rows1(bt):
                if not bt.there():
                    return
                pool.wait_ge(s_xnf, bt.count(2, 2))
                if (due := bt.by(-1).count(1, 1)) is not None:
                    pool.wait_ge(s_xt_full, due)
                cut(bt, XN[:, 0, :, :], XN[:, 1, :, :], XNF[:, :, :], s_xn, 2, 0)

            def rows2(bt):
                if not bt.there():
                    return
                pool.wait_ge(s_x2f, bt.count(2, 2))
                if (due := bt.by(-1).count(1, 1)) is not None:
                    pool.wait_ge(s_x2t_full, due)
                cut(bt, X2N[:, 0, :, :], X2N[:, 1, :, :], X2F[:, :, :], s_x2n, 2, 0)

            def stack_queries(bt):
                if not bt.there():
                    return
                g.memset(STILL[:, :], 0.0).then_inc(s_still, 1)
                if bt.fixed and bt.b < 2:
                    pool.wait_ge(s_zero, 2 * bt.b + 1)
                if (due := bt.by(-2).count(NCH, NCH)) is not None:
                    pool.wait_ge(s_sc_full, due)
                pool.wait_ge(s_qd, bt.count(2, 2))
                pool.wait_ge(s_still, bt.count(1, 1))
                apart(pool, bt)
                for j in range(4):
                    q = slice(32 * j, 32 * j + 32)
                    g.tensor_scalar(Z[bt.par][q, j, :, :], QD[q, :, :], 1.0, 0.0,
                                    ALU.mult, ALU.add).then_inc(s_z, 1)
                    pool.wait_ge(s_z, bt.count(4, j + 1))
                    apart(pool, bt)

            def residual(bt):
                if not bt.there():
                    return
                if bt.fixed and bt.b == 0:
                    pool.wait_ge(s_cst, 96)
                if (due := bt.by(-1).count(1, 1)) is not None:
                    pool.wait_ge(s_x2, due)
                pool.wait_ge(s_xb[bt.par], bt.half(16, 16))
                g.tensor_tensor(XBB[:, :, :], XB[bt.par][:, :, :], BR[:, 1:2, :].to_broadcast([P, NT, D]),
                                ALU.add).then_inc(s_xbb, 1)

            def hidden(bt):
                if not bt.there():
                    return
                pool.wait_ge(s_h, bt.count(4, 4))
                if (due := bt.by(-1).count(1, 1)) is not None:
                    pool.wait_ge(s_ht_full, due)
                src = HF[:, :, :].rearrange("p t (o i) -> p t o i", o=1).to_broadcast([P, NT, 2, NI])
                cut(bt, H16[:, 0, :, :, :], H16[:, 1, :, :, :], src, s_h16, 2, 0)

            def attention(bt):
                if not bt.there():
                    return
                pool.wait_ge(s_on, bt.count(3, 3))
                if (due := bt.by(-1).count(1, 1)) is not None:
                    pool.wait_ge(s_wo_full, due)
                cut(bt, OC16[:, 0, :], OC16[:, 1, :], OC[:, :], s_oc16, 2, 0)

            def qk(bt):
                if not bt.there():
                    return
                pool.wait_ge(s_qk, bt.count(3, 3))
                if (due := bt.by(-1).count(2, 2)) is not None:
                    pool.wait_ge(s_selk_full, due)
                if (due := bt.by(-1).count(1, 1)) is not None:
                    pool.wait_ge(s_self_full, due)
                if (due := bt.by(-1).count(2, 2)) is not None:
                    pool.wait_ge(s_selq_full, due)
                cut(bt, QK16[:, 0, :], QK16[:, 1, :], QKF[:, :], s_qk16, 2, 0)

            g.memset(HALF[:, :, :], -0.5).then_inc(s_half, 1)
            pool.wait_ge(s_half, 1)
            for p in range(2):
                g.memset(VS[p][:], 1.0).then_inc(s_ones, 1)

            def step_all(trip, u):
                i2, i1, i0, m1, m2 = [Batch(trip, u + k) for k in (2, 1, 0, -1, -2)]
                rows2(m2)
                residual(m1)
                qk(i1)
                stack_queries(i1)
                rstd1(i2)
                rows1(i2)
                attention(m1)
                hidden(m2)
                rstd2(m1)

            run(pool, step_all)


def kernel(L0_attn_hidden_states, L0_attn_Wq, L0_attn_bq, L0_attn_Wk, L0_attn_bk, L0_attn_Wv, L0_attn_bv,
           L0_attn_Wo, L0_attn_bo, L0_attn_dist_emb, L0_ffn_gate_w, L0_ffn_w_gate, L0_ffn_w_up, L0_ffn_w_down):
    import numpy as np
    import concourse.bacc as bacc
    from concourse.bass_utils import run_bass_kernel_spmd

    a = {k: np.asarray(v) for k, v in dict(
        x=L0_attn_hidden_states, wq=L0_attn_Wq, bq=L0_attn_bq, wk=L0_attn_Wk, bk=L0_attn_bk, wv=L0_attn_Wv,
        bv=L0_attn_bv, wo=L0_attn_Wo, bo=L0_attn_bo, dist=L0_attn_dist_emb, gw=L0_ffn_gate_w,
        wg=L0_ffn_w_gate, wu=L0_ffn_w_up, wd=L0_ffn_w_down).items()}

    wo_rows = a["wo"].T.reshape(NG, 4, C, D).transpose(1, 0, 2, 3).reshape(D, D)
    gu = np.stack([a["wg"], a["wu"]], 1).transpose(3, 0, 1, 2).reshape(D, NE * 2 * NI)
    wd = a["wd"].reshape(NE // 2, 2, D, NI).transpose(1, 3, 0, 2).reshape(2 * NI, (NE // 2) * D)
    w_all = np.concatenate([a["wq"].T, a["wk"].T, a["wv"].T, wo_rows, a["gw"].T, gu, wd], axis=1)
    biases = np.stack([a["bq"], a["bk"]], 1)
    edges = np.tile(a["dist"][[LEFT + RIGHT, 0]].T, (NH, 1))
    b_rows = np.broadcast_to(np.stack([a["bv"], a["bo"]])[None], (P, 2, D))
    at = np.clip(np.arange(TZW)[None, :] - XOFF - np.arange(4)[:, None], -LEFT, RIGHT) + LEFT
    dist_t = np.zeros((4, 4, C, TZW), a["dist"].dtype)
    dist_t[:, 0:3] = a["dist"][at].transpose(0, 2, 1)[:, None]
    dist0 = np.zeros((4, 4, C, 1), a["dist"].dtype)
    dist0[:, 0:3] = a["dist"][0][None, None, :, None]

    sel = np.zeros((NG, 4, C, 4, NG, 4, 4, C), np.float16)
    for g in range(NG):
        for j in range(4):
            for c in range(C):
                for operand, rows in ((0, (0, 1)), (1, (2,)), (2, (0, 2)), (3, (1,))):
                    for row in rows:
                        sel[g, j, c, operand, g, j, row, c] = 1
    kbias = np.zeros((4, 4, C, 1), np.float32)
    kbias[:, 3, 0] = MSCALE
    restrow = np.zeros((4, 4, C, 1), np.float32)
    restrow[:, 1] = -1
    iota = np.broadcast_to(np.arange(NE, dtype=np.float32), (P, NT, NE))
    arrays = {
        "x": a["x"], "w_all": w_all, "biases": biases, "edges": edges, "b_rows": b_rows,
        "dist_t": dist_t.reshape(P, TZW), "dist0": dist0.reshape(P, 1),
        "ident16": np.eye(P, dtype=np.float16), "ident32": np.eye(P, dtype=np.float32),
        "sel": sel.reshape(P, 4, NG, P), "kbias": kbias.reshape(P, 1), "restrow": restrow.reshape(P, 1),
        "iota": iota,
    }
    arrays = {k: np.ascontiguousarray(v) for k, v in arrays.items()}

    nc = bacc.Bacc("TRN2", target_bir_lowering=False, num_devices=1)
    args = [nc.dram_tensor(f"in_{k}", v.shape, mybir.dt.from_np(v.dtype), kind="ExternalInput").ap()
            for k, v in arrays.items()]
    out = nc.dram_tensor("out_0", (NB, L, D), F32, kind="ExternalOutput").ap()
    turned_q = nc.dram_tensor("turned_q", (2, 4, P, NG * L // 4), F16, kind="Internal").ap()
    build(nc, *args, turned_q, out)
    r = run_bass_kernel_spmd(nc, [{f"in_{k}": v for k, v in arrays.items()}], core_ids=[0])
    return r.results[0]["out_0"]
```

```python
from contextlib import ExitStack

import concourse.bass as bass
from concourse import mybir

ALU = mybir.AluOpType
ACT = mybir.ActivationFunctionType
F32 = mybir.dt.float32
F16 = mybir.dt.float16
AX_X = mybir.AxisListType.X

P = 128
NB = 16
L = 256
D = 128
NH = 16
C = 8
LEFT, RIGHT = 64, 8
NE = 8
NI = 64
NT = L // P
NG = 4
NCH = 16
QR = 32
NFAR = (P - RIGHT) // QR
NQK = 2 * L + P
SCALE = float(C) ** -0.5
EPS = 1e-5
MSCALE = 64.0
XOFF = L - 4
TZW = XOFF + L
WQ, WK, WV, WO, WG = 0, 128, 256, 384, 512
WGU = WG + NE
WD = WGU + NE * 2 * NI
WALL = WD + (NE // 2) * D

WARM_UPS = {
    ("x_turn", 0): 14, ("project_qk", 0): 3, ("queries", 0): 14, ("keys", 0): 1, ("max_chunk", 0): 16,
    ("max_chunk", 1): 18, ("h_turn", 14): 12, ("x2_turn", 15): 10, ("down", 14): 2, ("logits", 15): 2,
    ("experts", 15): 3, ("gate_up", 15): 17, ("h_turn", 15): 17, ("down", 15): 13,
}


class Batch:

    def __init__(self, trip, off):
        self.trip, self.off = trip, off
        self.par = off % 2
        self.fixed = isinstance(trip, int)

    @property
    def b(self):
        return self.trip * 2 + self.off

    def there(self):
        return not self.fixed or 0 <= self.b < NB

    def by(self, n):
        return Batch(self.trip, self.off + n)

    def count(self, per, k):
        n = self.trip * (2 * per) + (per * self.off + k)
        return None if self.fixed and (n <= 0 or self.b >= NB) else n

    def half(self, per, k):
        return self.trip * per + (per * (self.off // 2) + k) if self.there() else None


def build(nc, x, w_all, biases, edges, b_rows, dist_t, dist0, ident16, ident32, sel, kbias, restrow, iota,
          turned_q, out):
    with ExitStack() as ctx:
        def sb(name, shape, dt):
            return ctx.enter_context(nc.sbuf_tensor(name, shape, dt))

        def ps(name):
            return ctx.enter_context(nc.psum_tensor(name, [P, 512], F32))

        def sem(name):
            return ctx.enter_context(nc.semaphore(name))

        WF = sb("WF", [P, WALL], F32)
        W16 = sb("W16", [P, 2, WALL], F16)
        BI = sb("BI", [P, 2], F32)
        EDGE = sb("EDGE", [P, 2], F32)
        BFAR = sb("BFAR", [P, 2], F32)
        BR = sb("BR", [P, 2, D], F32)
        TF = sb("TF", [P, TZW], F32)
        TH = sb("TH", [P, TZW], F16)
        TZ = sb("TZ", [P, TZW], F16)
        D0 = sb("D0", [P, 1], F32)
        I16 = sb("I16", [P, P], F16)
        I32 = sb("I32", [P, P], F32)
        SEL = sb("SEL", [P, 4, NG, P], F16)
        KB = sb("KB", [P, 1], F32)
        RESTROW = sb("RESTROW", [P, 1], F32)
        IOTA = sb("IOTA", [P, NT, NE], F32)
        XF = [sb(f"XF{p}", [P, NT, D], F32) for p in range(2)]
        ST1 = sb("ST1", [P, NT, 6], F32)
        MV1 = sb("MV1", [P, NT, 2], F32)
        VE1 = sb("VE1", [P, NT, 1], F32)
        WARM = sb("WARM", [P, 512], F16)
        STILL = sb("STILL", [P, 1], F32)
        TABLE = sb("TABLE", [P, NT, 1], F32)
        HALF = sb("HALF", [P, NT, 1], F32)
        RS1 = sb("RS1", [P, NT, 1], F32)
        XNF = sb("XNF", [P, NT, D], F32)
        XN = sb("XN", [P, 2, NT, D], F16)
        XT = sb("XT", [P, 2, L], F16)
        QKF = sb("QKF", [P, NQK], F32)
        QK16 = sb("QK16", [P, 2, NQK], F16)
        QD = sb("QD", [P, NG, L], F16)
        QP = sb("QP", [P, 4, NG, L // 4], F16)
        K4 = [sb(f"K4{p}", [P, NG, L], F16) for p in range(2)]
        KF = [sb(f"KF{p}", [P, NG, P], F16) for p in range(2)]
        Z = [sb(f"Z{p}", [P, 4, NG, L], F16) for p in range(2)]
        R = [sb(f"R{p}", [P, 4, NH, L // 4], F16) for p in range(2)]
        VS = [sb(f"VS{p}", [P, NT, NH, QR], F32) for p in range(2)]
        MXR = sb("MXR", [P, NT, P], F32)
        MXC = sb("MXC", [P, P], F32)
        MN = sb("MN", [P, QR], F32)
        M16 = sb("M16", [P, QR], F16)
        PT = [sb(f"PT{p}", [P, NT, NH, L], F32) for p in range(2)]
        OT = sb("OT", [P, NG, 8, QR], F32)
        RD = sb("RD", [P, NG, 8], F32)
        ON = sb("ON", [P, 8, NG, C], F32)
        OC = sb("OC", [P, L], F32)
        OC16 = sb("OC16", [P, 2, L], F16)
        XB = [sb(f"XB{p}", [P, NT, D], F32) for p in range(2)]
        XBB = sb("XBB", [P, NT, D], F32)
        X2 = [sb(f"X2{p}", [P, NT, D], F32) for p in range(2)]
        ST2 = sb("ST2", [P, NT, 6], F32)
        MV2 = sb("MV2", [P, NT, 2], F32)
        VE2 = sb("VE2", [P, NT, 1], F32)
        RS2 = sb("RS2", [P, NT, 1], F32)
        X2F = sb("X2F", [P, NT, D], F32)
        X2N = sb("X2N", [P, 2, NT, D], F16)
        X2T = sb("X2T", [P, 2, L], F16)
        LMX = sb("LMX", [P, NT], F32)
        LLT = sb("LLT", [P, NT, NE], F32)
        LIX = sb("LIX", [P, NT, NE], F32)
        LID = sb("LID", [P, NT], F16)
        EID = sb("EID", [P, L], F16)
        REX = sb("REX", [P, NT], F32)
        RP1 = sb("RP1", [P, NT], F32)
        RW = sb("RW", [P, NT], F32)
        MK = sb("MK", [P, NE, L], F16)
        XM = sb("XM", [P, 2, NE, L], F16)
        GUF = sb("GUF", [P, NT, 2, NI], F32)
        GE = sb("GE", [P, NT, NI], F32)
        GP = sb("GP", [P, NT, NI], F32)
        GR = sb("GR", [P, NT, NI], F32)
        GS = sb("GS", [P, NT, NI], F32)
        HF = sb("HF", [P, NT, NI], F32)
        H16 = sb("H16", [P, 2, NT, 2, NI], F16)
        HT = sb("HT", [P, 2, L], F16)
        HM = sb("HM", [P, 2, NE // 2, L], F16)
        Y = [sb(f"Y{p}", [P, NT, D], F32) for p in range(2)]

        MX = [ps("MX0"), ps("MX1")]
        SC = [ps("SC0"), ps("SC1")]
        PO = ps("PO")
        BA, BB, BC = ps("BA"), ps("BB"), ps("BC")

        s_cst = sem("s_cst")
        s_wqkvo = sem("s_wqkvo")
        s_wld = sem("s_wld")
        s_zero = sem("s_zero")
        s_ones = sem("s_ones")
        s_w16 = sem("s_w16")
        s_tz = sem("s_tz")
        s_warm = sem("s_warm")
        s_half = sem("s_half")
        s_apart = sem("s_apart")
        s_xf = [sem(f"s_xf{p}") for p in range(2)]
        s_xb = [sem(f"s_xb{p}") for p in range(2)]
        s_r = [sem(f"s_r{p}") for p in range(2)]
        s_qpd = [sem(f"s_qpd{p}") for p in range(2)]
        s_m = [sem(f"s_m{p}") for p in range(2)]
        s_y = [sem(f"s_y{p}") for p in range(2)]
        s_ln1 = sem("s_ln1")
        s_rs1 = sem("s_rs1")
        s_xnf = sem("s_xnf")
        s_xn = sem("s_xn")
        s_xt_full = sem("s_xt_full")
        s_xt = sem("s_xt")
        s_qk_full = sem("s_qk_full")
        s_qk = sem("s_qk")
        s_qk16 = sem("s_qk16")
        s_selk_full = sem("s_selk_full")
        s_k4 = sem("s_k4")
        s_self_full = sem("s_self_full")
        s_kf = sem("s_kf")
        s_selq_full = sem("s_selq_full")
        s_qd = sem("s_qd")
        s_qp = sem("s_qp")
        s_z = sem("s_z")
        s_still = sem("s_still")
        s_v_full = sem("s_v_full")
        s_v = sem("s_v")
        s_mx_full = sem("s_mx_full")
        s_tr = sem("s_tr")
        s_mxc = sem("s_mxc")
        s_mt_full = sem("s_mt_full")
        s_m16 = sem("s_m16")
        s_sc_full = sem("s_sc_full")
        s_exp = sem("s_exp")
        s_pv_full = sem("s_pv_full")
        s_ot = sem("s_ot")
        s_on = sem("s_on")
        s_oc16 = sem("s_oc16")
        s_xbb = sem("s_xbb")
        s_wo_full = sem("s_wo_full")
        s_x2 = sem("s_x2")
        s_ln2 = sem("s_ln2")
        s_rs2 = sem("s_rs2")
        s_x2f = sem("s_x2f")
        s_x2n = sem("s_x2n")
        s_x2t_full = sem("s_x2t_full")
        s_x2t = sem("s_x2t")
        s_lg_full = sem("s_lg_full")
        s_gate = sem("s_gate")
        s_rex = sem("s_rex")
        s_rw = sem("s_rw")
        s_eid_full = sem("s_eid_full")
        s_eid = sem("s_eid")
        s_mk = sem("s_mk")
        s_xm = sem("s_xm")
        s_gu_full = sem("s_gu_full")
        s_guf = sem("s_guf")
        s_ge = sem("s_ge")
        s_h = sem("s_h")
        s_h16 = sem("s_h16")
        s_ht_full = sem("s_ht_full")
        s_ht = sem("s_ht")
        s_hm = sem("s_hm")
        s_dn_full = sem("s_dn_full")
        s_yf = sem("s_yf")
        s_table = sem("s_table")
        s_bfar = sem("s_bfar")

        def apart(eng, bt):
            if not bt.fixed:
                eng.sem_inc(s_apart, 1)

        def run(eng, step_all):
            for i in range(-2, 4):
                step_all(i // 2, i % 2)
            with eng.Fori(2, 6) as trip:
                for u in range(2):
                    step_all(trip, u)
            for i in range(12, 18):
                step_all(i // 2, i % 2)

        block = ctx.enter_context(nc.Block())

        @block.sync
        def _(sp):
            def load_xf(bt):
                if not bt.there():
                    return
                prev = Batch(bt.trip, bt.off - 2)
                if (due := prev.count(2, 2)) is not None:
                    sp.wait_ge(s_xnf, due)
                apart(sp, bt)
                sp.dma_start(XF[bt.par][:, :, :], x[bass.ds(bt.b, 1), :, :].rearrange(
                    "o (t p) d -> p (o t) d", p=P)).then_inc(s_xf[bt.par], 16)

            def load_xb(bt):
                if not bt.there():
                    return
                if (due := bt.by(-2).count(1, 1)) is not None:
                    sp.wait_ge(s_xbb, due)
                apart(sp, bt)
                sp.dma_start(XB[bt.par][:, :, :], x[bass.ds(bt.b, 1), :, :].rearrange(
                    "o (t p) d -> p (o t) d", p=P)).then_inc(s_xb[bt.par], 16)

            load_xf(Batch(0, 0))
            sp.dma_start(WF[:, 0:WGU], w_all[:, 0:WGU]).then_inc(s_wqkvo, 16)
            for dst, src in ((I16, ident16), (SEL, sel), (KB, kbias), (BI, biases), (EDGE, edges), (BR, b_rows)):
                sp.dma_start(dst[:], src).then_inc(s_cst, 16)
            load_xf(Batch(0, 1))
            for dst, src in ((TF, dist_t), (D0, dist0), (RESTROW, restrow), (I32, ident32), (IOTA, iota)):
                sp.dma_start(dst[:], src).then_inc(s_wld, 16)
            sp.dma_start(WF[:, WGU:WALL], w_all[:, WGU:WALL]).then_inc(s_wld, 16)

            def step_all(trip, u):
                nxt, last, cur, nxt3 = Batch(trip, u + 1), Batch(trip, u - 1), Batch(trip, u), Batch(trip, u + 3)
                if nxt.there():
                    if (due := last.count(NCH, NCH)) is not None:
                        sp.wait_ge(s_sc_full, due)
                        apart(sp, nxt)
                    if nxt.fixed and nxt.b < 2:
                        sp.wait_ge(s_zero, 2 * nxt.b + 2)
                    sp.wait_ge(s_qpd[nxt.par], nxt.half(16, 16))
                    apart(sp, nxt)
                    for a in range(4):
                        sp.dma_start(R[nxt.par][32 * a:32 * a + 32, a, :, :].rearrange(
                            "p (j g) q -> p j (g q)", j=4),
                            turned_q[nxt.par, a].rearrange("(j p) x -> p j x", j=4)).then_inc(s_r[nxt.par], 16)
                if nxt3.there() and not (nxt3.fixed and nxt3.b < 2):
                    load_xf(nxt3)
                if cur.there():
                    load_xb(cur)
                late = Batch(trip, u - 2)
                if late.there():
                    sp.wait_ge(s_yf, late.count(1, 1))
                    apart(sp, late)
                    sp.dma_start(out[bass.ds(late.b, 1), :, :].rearrange("o (t p) d -> p (o t) d", p=P),
                                 Y[late.par][:, :, :]).then_inc(s_y[late.par], 16)
                nxt2 = Batch(trip, u + 2)
                if nxt2.there():
                    if (due := nxt2.by(-2).half(64, 64)) is not None:
                        sp.wait_ge(s_r[nxt2.par], due)
                        apart(sp, nxt2)
                    sp.wait_ge(s_qp, nxt2.count(2, 2))
                    apart(sp, nxt2)
                    sp.dma_start(turned_q[nxt2.par].rearrange("a p x -> p a x"),
                                 QP[:, :, :, :].rearrange("p a g q -> p a (g q)")).then_inc(s_qpd[nxt2.par], 16)
                if nxt.there():
                    sp.wait_ge(s_m16, nxt.count(2, 2))
                    apart(sp, nxt)
                    sp.wait_ge(s_z, nxt.count(4, 4))
                    for j in range(4):
                        row = 32 * j + 3 * C
                        sp.dma_start(Z[nxt.par][row:row + 1, j, :, :].rearrange("o g (b l) -> o (g b) l", l=QR),
                                     M16[32 * j:32 * j + 32, :]).then_inc(s_m[nxt.par], 16)

            run(sp, step_all)
            for par in range(2):
                sp.wait_ge(s_y[par], 16 * NB // 2)

        @block.tensor
        def _(pe):
            mm = nc.tensor.matmul

            def warm_up(stage, bt):
                for _ in range(WARM_UPS.get((stage, bt.b), 0) if bt.fixed else 0):
                    mm(MX[1][:, :], WARM[:, 0:P], WARM[:, :], start=True, stop=True)

            def three(out_ap, stat, mov, start, stop):
                mm(out_ap, stat(0), mov(0), start=start, stop=False, skip_group_check=True)
                mm(out_ap, stat(0), mov(1), start=False, stop=False, skip_group_check=True)
                return mm(out_ap, stat(1), mov(0), start=False, stop=stop, skip_group_check=True)

            def chunk(bank, bt, n):
                lb, rt = n // 2, n % 2
                groups = [q for q in range(8 * lb, 8 * lb + 8)
                          if not (rt + 1) * P - 1 <= 4 * q - LEFT]
                far = rt == 1 and lb < NFAR
                if far:
                    groups = []
                for g in range(NG):
                    keys_of = KF[bt.par][:, g, :] if far else K4[bt.par][:, g, P * rt:P * rt + P]
                    last = mm(bank[:, P * g:P * g + P], keys_of,
                              Z[bt.par][:, :, g, QR * lb:QR * lb + QR],
                              start=g == 0, stop=g == NG - 1 and not groups, skip_group_check=True)
                outs = bank[:, :].rearrange("p (g j q a) -> p g j q a", g=NG, j=4, a=4)
                rel = R[bt.par][:, :, :, :].rearrange("p a (j g) q -> p g j a q", j=4)
                for q in groups:
                    at = XOFF + P * rt - 4 * q
                    last = mm(outs[:, :, :, q - 8 * lb, :], TZ[:, at:at + P], rel[:, :, :, :, q],
                              start=False, stop=q == groups[-1], skip_group_check=True)
                return last

            def max_chunk(bt, n):
                if not bt.there():
                    return
                if n == 0:
                    warm_up("max_chunk", bt)
                if n == 0:
                    pe.wait_ge(s_z, bt.count(4, 4))
                    pe.wait_ge(s_r[bt.par], bt.half(64, 64))
                    pe.wait_ge(s_k4, bt.count(2, 2))
                    pe.wait_ge(s_kf, bt.count(1, 1))
                    if bt.fixed and bt.b == 0:
                        pe.wait_ge(s_tz, 3)
                if (due := bt.count(NCH, n - 1)) is not None:
                    pe.wait_ge(s_tr, due)
                chunk(MX[n % 2], bt, n).then_inc(s_mx_full, 1)

            def score_chunk(bt, n):
                if not bt.there():
                    return
                if n == 0:
                    pe.wait_ge(s_m[bt.par], bt.half(64, 64))
                if (due := bt.count(NCH, n - 1)) is not None:
                    pe.wait_ge(s_exp, due)
                chunk(SC[n % 2], bt, n).then_inc(s_sc_full, 1)

            def select(bank, kind, tokens, groups, full):
                wide = tokens.stop - tokens.start
                for n, g in enumerate(groups):
                    o = bank[:, wide * n:wide * n + wide]
                    mm(o, SEL[:, 2 * kind, g, :], QK16[:, 0, tokens], start=True, stop=False)
                    last = mm(o, SEL[:, 2 * kind + 1, g, :], QK16[:, 1, tokens], start=False, stop=True)
                last.then_inc(full, 1)

            def keys_far(bt):
                if not bt.there():
                    return
                pe.wait_ge(s_qk16, bt.count(2, 2))
                if (due := bt.by(-3).count(1, 1)) is not None:
                    pe.wait_ge(s_eid, due)
                if (due := bt.by(-1).count(1, 1)) is not None:
                    pe.wait_ge(s_kf, due)
                select(BB, 1, slice(2 * L, NQK), range(NG), s_self_full)

            def keys(bt):
                if not bt.there():
                    return
                warm_up("keys", bt)
                pe.wait_ge(s_qk16, bt.count(2, 2))
                pe.wait_ge(s_qd, bt.count(2, 2))
                if (due := bt.by(-1).count(2, 1)) is not None:
                    pe.wait_ge(s_m16, due)
                select(BA, 1, slice(L, 2 * L), (0, 1), s_selk_full)
                select(BC, 1, slice(L, 2 * L), (2, 3), s_selk_full)

            def pv(bt, half):
                if not bt.there():
                    return
                if half == 0:
                    pe.wait_ge(s_v, bt.count(1, 1))
                    pe.wait_ge(s_exp, bt.count(NCH, NCH))
                if (due := bt.count(2, half)) is not None:
                    pe.wait_ge(s_ot, due)
                for gg in range(2):
                    for rt in range(NT):
                        for j in range(4):
                            h = 4 * (2 * half + gg) + j
                            last = mm(PO[32 * j:32 * j + 32, L * gg:L * gg + L], VS[bt.par][:, rt, h, :],
                                      PT[bt.par][:, rt, h, :], start=rt == 0, stop=rt == NT - 1,
                                      skip_group_check=True)
                last.then_inc(s_pv_full, 1)

            def values(bt):
                if not bt.there():
                    return
                pe.wait_ge(s_k4, bt.count(2, 2))
                for t in range(NT):
                    last = three(BC[:, D * t:D * t + D], lambda s: XT[:, s, P * t:P * t + P],
                                 lambda s: W16[:, s, WV:WV + D], True, True)
                last.then_inc(s_v_full, 1)

            def turn(bank, src, full):
                o = bank[:, 0:2 * P].bitcast(F16)
                for s in range(2):
                    for t in range(NT):
                        c = (s * NT + t) * P
                        last = nc.tensor.transpose(o[:, c:c + P], src(s, t), I16[:, :])
                last.then_inc(full, 1)

            def h_turn(bt):
                if not bt.there():
                    return
                warm_up("h_turn", bt)
                pe.wait_ge(s_h16, bt.count(2, 2))
                pe.wait_ge(s_eid, bt.count(1, 1))
                if (due := bt.by(1).count(1, 1)) is not None:
                    pe.wait_ge(s_x2, due)
                turn(BB, lambda s, t: H16[:, s, t, :, :].rearrange("p a i -> p (a i)"), s_ht_full)

            def x_turn(bt):
                if not bt.there():
                    return
                warm_up("x_turn", bt)
                if bt.fixed and bt.b == 0:
                    pe.wait_ge(s_cst, 96)
                pe.wait_ge(s_xn, bt.count(2, 2))
                if (due := bt.by(-1).count(2, 1)) is not None:
                    pe.wait_ge(s_k4, due)
                if (due := bt.by(-4).count(1, 1)) is not None:
                    pe.wait_ge(s_guf, due)
                turn(BA, lambda s, t: XN[:, s, t, :], s_xt_full)

            def project_out(bt):
                if not bt.there():
                    return
                pe.wait_ge(s_oc16, bt.count(2, 2))
                if (due := bt.by(-1).count(1, 1)) is not None:
                    pe.wait_ge(s_eid, due)
                if (due := bt.by(2).count(1, 1)) is not None:
                    pe.wait_ge(s_kf, due)
                for t in range(NT):
                    last = three(BB[:, D * t:D * t + D], lambda s: OC16[:, s, P * t:P * t + P],
                                 lambda s: W16[:, s, WO:WO + D], True, True)
                last.then_inc(s_wo_full, 1)

            def project_qk(bt):
                if not bt.there():
                    return
                warm_up("project_qk", bt)
                if bt.fixed and bt.b == 0:
                    pe.wait_ge(s_w16, 2)
                pe.wait_ge(s_xt, bt.count(1, 1))
                for kind, w in enumerate((WQ, WK)):
                    last = three(BA[:, L * kind:L * kind + L], lambda s: W16[:, s, w:w + D],
                                 lambda s: XT[:, s, :], True, True)
                last.then_inc(s_qk_full, 1)

            def down(bt):
                if not bt.there():
                    return
                warm_up("down", bt)
                pe.wait_ge(s_hm, bt.count(2, 2))
                for t in range(NT):
                    for e in range(NE // 2):
                        last = three(BB[:, D * t:D * t + D], lambda s: HM[:, s, e, P * t:P * t + P],
                                     lambda s: W16[:, s, WD + D * e:WD + D * e + D], e == 0, e == NE // 2 - 1)
                last.then_inc(s_dn_full, 1)

            def x2_turn(bt):
                if not bt.there():
                    return
                warm_up("x2_turn", bt)
                pe.wait_ge(s_x2n, bt.count(2, 2))
                if (due := bt.by(2).count(1, 1)) is not None:
                    pe.wait_ge(s_v, due)
                turn(BC, lambda s, t: X2N[:, s, t, :], s_x2t_full)

            def queries(bt, half):
                if not bt.there():
                    return
                if half == 0:
                    warm_up("queries", bt)
                if half == 0:
                    pe.wait_ge(s_qk16, bt.count(2, 2))
                    select(BA, 0, slice(0, L), (0, 1), s_selq_full)
                else:
                    if (due := bt.by(-1).count(1, 1)) is not None:
                        pe.wait_ge(s_v, due)
                    if (due := bt.by(-3).count(1, 1)) is not None:
                        pe.wait_ge(s_x2t, due)
                    select(BC, 0, slice(0, L), (2, 3), s_selq_full)

            def logits(bt):
                if not bt.there():
                    return
                warm_up("logits", bt)
                pe.wait_ge(s_x2t, bt.count(1, 1))
                if (due := bt.by(-1).count(1, 1)) is not None:
                    pe.wait_ge(s_yf, due)
                for t in range(NT):
                    last = three(BB[:, NE * t:NE * t + NE], lambda s: X2T[:, s, P * t:P * t + P],
                                 lambda s: W16[:, s, WG:WG + NE], True, True)
                last.then_inc(s_lg_full, 1)

            def max_turn(bt):
                if not bt.there():
                    return
                if bt.fixed and bt.b == 0:
                    pe.wait_ge(s_wld, 96)
                pe.wait_ge(s_mxc, bt.count(1, 1))
                if (due := bt.by(1).count(2, 1)) is not None:
                    pe.wait_ge(s_qd, due)
                nc.tensor.transpose(BA[:, 0:P], MXC[:, :], I32[:, :]).then_inc(s_mt_full, 1)

            def experts(bt):
                if not bt.there():
                    return
                warm_up("experts", bt)
                pe.wait_ge(s_gate, bt.count(4, 4))
                for t in range(NT):
                    last = mm(BB[:, P * t:P * t + P], LID[:, t:t + 1].to_broadcast([P, P]), I16[:, :],
                              start=True, stop=True)
                last.then_inc(s_eid_full, 1)

            def gate_up(bt):
                if not bt.there():
                    return
                warm_up("gate_up", bt)
                if bt.fixed and bt.b == 0:
                    pe.wait_ge(s_w16, 4)
                pe.wait_ge(s_xm, bt.count(2, 2))
                if (due := bt.by(2).count(2, 1)) is not None:
                    pe.wait_ge(s_m16, due)
                if (due := bt.by(3).count(2, 1)) is not None:
                    pe.wait_ge(s_k4, due)
                for t in range(NT):
                    for e in range(NE):
                        last = three(BA[:, D * t:D * t + D], lambda s: XM[:, s, e, P * t:P * t + P],
                                     lambda s: W16[:, s, WGU + 2 * NI * e:WGU + 2 * NI * (e + 1)],
                                     e == 0, e == NE - 1)
                last.then_inc(s_gu_full, 1)

            pe.wait_ge(s_warm, 1)

            def step_all(trip, u):
                i2, i1, i0, m1, m2 = [Batch(trip, u + k) for k in (2, 1, 0, -1, -2)]
                score_chunk(m1, 14)
                max_chunk(i0, 15)
                score_chunk(m1, 15)
                queries(i1, 1)
                experts(m2)
                max_turn(i0)
                pv(m1, 0)
                keys(i1)
                keys_far(i1)
                pv(m1, 1)
                values(i1)
                gate_up(m2)
                max_chunk(i1, 0)
                max_chunk(i1, 1)
                score_chunk(i0, 0)
                score_chunk(i0, 1)
                max_chunk(i1, 2)
                max_chunk(i1, 3)
                score_chunk(i0, 2)
                score_chunk(i0, 3)
                project_out(m1)
                x_turn(i2)
                max_chunk(i1, 4)
                score_chunk(i0, 4)
                max_chunk(i1, 5)
                score_chunk(i0, 5)
                project_qk(i2)
                max_chunk(i1, 6)
                score_chunk(i0, 6)
                max_chunk(i1, 7)
                h_turn(m2)
                max_chunk(i1, 8)
                score_chunk(i0, 7)
                max_chunk(i1, 9)
                score_chunk(i0, 8)
                score_chunk(i0, 9)
                max_chunk(i1, 10)
                score_chunk(i0, 10)
                x2_turn(m1)
                max_chunk(i1, 11)
                score_chunk(i0, 11)
                score_chunk(i0, 12)
                down(m2)
                max_chunk(i1, 12)
                max_chunk(i1, 13)
                score_chunk(i0, 13)
                queries(i2, 0)
                logits(m1)
                max_chunk(i1, 14)

            run(pe, step_all)

        @block.scalar
        def _(act):
            copy = nc.scalar.activation

            def exps(bt, n):
                if not bt.there():
                    return
                lb, rt = n // 2, n % 2
                if n == 0:
                    if (due := bt.by(-2).count(2, 2)) is not None:
                        act.wait_ge(s_pv_full, due)
                act.wait_ge(s_sc_full, bt.count(NCH, n + 1))
                copy(PT[bt.par][:, rt, :, QR * lb:QR * lb + QR],
                     SC[n % 2][:, :].rearrange("p (h l) -> p h l", h=NH), ACT.Exp,
                     scale=SCALE).then_inc(s_exp, 1)

            def keys(bt):
                if not bt.there():
                    return
                if (due := bt.by(-2).count(NCH, NCH)) is not None:
                    act.wait_ge(s_sc_full, due)
                for half, bank in enumerate((BA, BC)):
                    act.wait_ge(s_selk_full, bt.count(2, half + 1))
                    copy(K4[bt.par][:, 2 * half:2 * half + 2, :],
                         bank[:, :].rearrange("p (g l) -> p g l", g=2), ACT.Identity,
                         bias=KB[:, 0:1]).then_inc(s_k4, 1)

            def keys_far(bt):
                if not bt.there():
                    return
                if (due := bt.by(-2).count(NCH, NCH)) is not None:
                    act.wait_ge(s_sc_full, due)
                act.wait_ge(s_self_full, bt.count(1, 1))
                copy(KF[bt.par][:, :, :], BB[:, :].rearrange("p (g l) -> p g l", g=NG), ACT.Identity,
                     bias=KB[:, 0:1]).then_inc(s_kf, 1)

            def queries(bt, half):
                if not bt.there():
                    return
                if half == 0:
                    if (due := bt.by(-1).count(4, 4)) is not None:
                        act.wait_ge(s_z, due)
                    if (due := bt.by(-1).half(16, 16)) is not None:
                        act.wait_ge(s_qpd[1 - bt.par], due)
                act.wait_ge(s_selq_full, bt.count(2, half + 1))
                copy(QP[:, :, 2 * half:2 * half + 2, :],
                     (BA, BC)[half][:, :].rearrange("p (g q a) -> p a g q", g=2, a=4),
                     ACT.Copy).then_inc(s_qp, 1)
                copy(QD[:, 2 * half:2 * half + 2, :],
                     (BA, BC)[half][:, :].rearrange("p (g l) -> p g l", g=2),
                     ACT.Copy).then_inc(s_qd, 1)

            def turned(bank):
                return bank[:, 0:2 * P].bitcast(F16).rearrange("p (s l) -> p s l", s=2)

            def turned_x1(bt):
                if not bt.there():
                    return
                if (due := bt.by(-1).count(1, 1)) is not None:
                    act.wait_ge(s_v_full, due)
                act.wait_ge(s_xt_full, bt.count(1, 1))
                copy(XT[:, :, :], turned(BA), ACT.Copy).then_inc(s_xt, 1)

            def turned_x2(bt):
                if not bt.there():
                    return
                if (due := bt.by(-1).count(2, 2)) is not None:
                    act.wait_ge(s_xm, due)
                act.wait_ge(s_x2t_full, bt.count(1, 1))
                copy(X2T[:, :, :], turned(BC), ACT.Copy).then_inc(s_x2t, 1)

            def turned_h(bt):
                if not bt.there():
                    return
                if (due := bt.by(-1).count(2, 2)) is not None:
                    act.wait_ge(s_hm, due)
                act.wait_ge(s_ht_full, bt.count(1, 1))
                copy(HT[:, :, :], turned(BB), ACT.Copy).then_inc(s_ht, 1)

            def qk(bt):
                if not bt.there():
                    return
                if (due := bt.by(-1).count(2, 2)) is not None:
                    act.wait_ge(s_qk16, due)
                act.wait_ge(s_qk_full, bt.count(1, 1))
                for kind in range(2):
                    copy(QKF[:, L * kind:L * kind + L], BA[:, L * kind:L * kind + L], ACT.Identity,
                         bias=BI[:, kind:kind + 1]).then_inc(s_qk, 1)
                if bt.fixed and bt.b == 0:
                    act.wait_ge(s_bfar, 2)
                copy(QKF[:, 2 * L:NQK], BA[:, L + P:2 * L], ACT.Identity, bias=BFAR[:, 1:2]).then_inc(s_qk, 1)

            def experts(bt):
                if not bt.there():
                    return
                if (due := bt.by(-1).count(NE, NE)) is not None:
                    act.wait_ge(s_mk, due)
                act.wait_ge(s_eid_full, bt.count(1, 1))
                copy(EID[:, :], BB[:, 0:L], ACT.Copy).then_inc(s_eid, 1)

            def weight_exp(bt):
                if not bt.there():
                    return
                if (due := bt.by(-1).count(2, 2)) is not None:
                    act.wait_ge(s_rex, due)
                act.wait_ge(s_gate, bt.count(4, 1))
                copy(REX[:, :], LMX[:, :], ACT.Exp, scale=-1.0).then_inc(s_rex, 1)

            def gate_exp(bt):
                if not bt.there():
                    return
                if (due := bt.by(-1).count(2, 2)) is not None:
                    act.wait_ge(s_ge, due)
                act.wait_ge(s_guf, bt.count(1, 1))
                copy(GE[:, :, :], GUF[:, :, 0, :], ACT.Exp, scale=-1.0).then_inc(s_ge, 1)

            def gate_sum(bt):
                if not bt.there():
                    return
                if (due := bt.by(-1).count(3, 1)) is not None:
                    act.wait_ge(s_h, due)
                act.wait_ge(s_ge, bt.count(2, 1))
                copy(GP[:, :, :], GE[:, :, :], ACT.Identity, bias=1.0).then_inc(s_ge, 1)

            def weight_sum(bt):
                if not bt.there():
                    return
                if (due := bt.by(-1).count(1, 1)) is not None:
                    act.wait_ge(s_rw, due)
                act.wait_ge(s_rex, bt.count(2, 1))
                copy(RP1[:, :], REX[:, :], ACT.Identity, bias=1.0).then_inc(s_rex, 1)

            act.wait_ge(s_half, 1)
            copy(TABLE[:, :, :], HALF[:, :, :], ACT.Exp).then_inc(s_table, 1)
            act.wait_ge(s_cst, 96)

            def step_all(trip, u):
                i2, i1, i0, m1, m2 = [Batch(trip, u + k) for k in (2, 1, 0, -1, -2)]
                exps(m1, 14)
                weight_exp(m2)
                exps(m1, 15)
                weight_sum(m2)
                queries(i1, 1)
                experts(m2)
                keys(i1)
                keys_far(i1)
                gate_exp(m2)
                gate_sum(m2)
                exps(i0, 0)
                exps(i0, 1)
                exps(i0, 2)
                exps(i0, 3)
                turned_x1(i2)
                exps(i0, 4)
                exps(i0, 5)
                qk(i2)
                exps(i0, 6)
                turned_h(m2)
                exps(i0, 7)
                exps(i0, 8)
                exps(i0, 9)
                exps(i0, 10)
                exps(i0, 11)
                turned_x2(m1)
                exps(i0, 12)
                exps(i0, 13)
                queries(i2, 0)

            run(act, step_all)

        @block.vector
        def _(dve):
            v = nc.vector

            def ln1_stats(bt):
                if not bt.there():
                    return
                if (due := bt.by(-1).count(4, 4)) is not None:
                    dve.wait_ge(s_ln1, due)
                dve.wait_ge(s_xf[bt.par], bt.half(16, 16))
                for t in range(NT):
                    v.bn_stats(ST1[:, t, :], XF[bt.par][:, t, :]).then_inc(s_ln1, 1)

            def ln1_aggregate(bt):
                if not bt.there():
                    return
                if (due := bt.by(-1).count(2, 2)) is not None:
                    dve.wait_ge(s_xnf, due)
                dve.wait_ge(s_ln1, bt.count(4, 2))
                apart(dve, bt)
                for t in range(NT):
                    v.bn_aggr(MV1[:, t, :], ST1[:, t, :]).then_inc(s_ln1, 1)

            def normalise(bt, src, mv, rs, full, done):
                for t in range(NT):
                    v.tensor_scalar(full[:, t, :], src[:, t, :], mv[:, t, 0:1], rs[:, t, :],
                                    ALU.subtract, ALU.mult).then_inc(done, 1)

            def far_bias():
                dve.wait_ge(s_cst, 96)
                v.tensor_tensor(BFAR[:, 0:1], EDGE[:, 0:1], EDGE[:, 1:2], ALU.subtract).then_inc(s_bfar, 1)
                dve.wait_ge(s_bfar, 1)
                v.tensor_tensor(BFAR[:, 1:2], BFAR[:, 0:1], BI[:, 1:2], ALU.add).then_inc(s_bfar, 1)

            def cut_projections():
                dve.wait_ge(s_wqkvo, 16)
                v.tensor_copy(W16[:, 0, 0:WGU], WF[:, 0:WGU]).then_inc(s_w16, 1)
                dve.wait_ge(s_w16, 1)
                v.tensor_tensor(W16[:, 1, 0:WGU], WF[:, 0:WGU], W16[:, 0, 0:WGU], ALU.subtract).then_inc(s_w16, 1)

            def other_constants():
                v.memset(R[0][:], 0.0).then_inc(s_zero, 1)
                dve.wait_ge(s_wld, 96)
                v.tensor_scalar(TF[:, :], TF[:, :], D0[:, 0:1], None, ALU.subtract).then_inc(s_tz, 1)
                dve.wait_ge(s_tz, 1)
                v.tensor_copy(TH[:, :], TF[:, :]).then_inc(s_tz, 1)
                dve.wait_ge(s_tz, 2)
                v.scalar_tensor_tensor(TZ[:, :], TH[:, :], RESTROW[:, 0:1], TF[:, :],
                                       ALU.mult, ALU.add).then_inc(s_tz, 1)
                v.memset(Z[1][:], 0.0).then_inc(s_zero, 1)
                v.memset(R[1][:], 0.0).then_inc(s_zero, 1)
                v.tensor_copy(W16[:, 0, WGU:WALL], WF[:, WGU:WALL]).then_inc(s_w16, 1)
                dve.wait_ge(s_w16, 3)
                v.tensor_tensor(W16[:, 1, WGU:WALL], WF[:, WGU:WALL], W16[:, 0, WGU:WALL],
                                ALU.subtract).then_inc(s_w16, 1)

            def norm1(bt):
                if not bt.there():
                    return
                if bt.fixed and bt.b == 0:
                    cut_projections()
                dve.wait_ge(s_rs1, bt.count(2, 2))
                if (due := bt.by(-1).count(2, 2)) is not None:
                    dve.wait_ge(s_xn, due)
                apart(dve, bt)
                normalise(bt, XF[bt.par], MV1, RS1, XNF, s_xnf)
                if bt.fixed and bt.b == 0:
                    far_bias()
                    other_constants()

            def norm2(bt):
                if not bt.there():
                    return
                dve.wait_ge(s_rs2, bt.count(2, 2))
                if (due := bt.by(-1).count(2, 2)) is not None:
                    dve.wait_ge(s_x2n, due)
                apart(dve, bt)
                normalise(bt, X2[bt.par], MV2, RS2, X2F, s_x2f)

            def gates_scale(bt):
                if not bt.there():
                    return
                dve.wait_ge(s_gu_full, bt.count(1, 1))
                dve.wait_ge(s_rw, bt.count(1, 1))
                if (due := bt.by(-1).count(2, 1)) is not None:
                    dve.wait_ge(s_ge, due)
                if (due := bt.by(-1).count(3, 3)) is not None:
                    dve.wait_ge(s_h, due)
                v.tensor_tensor(GUF[:, :, :, :].rearrange("p t a i -> p t (a i)"),
                                BA[:, 0:NT * D].rearrange("p (t d) -> p t d", t=NT),
                                RW[:, :].rearrange("p (t o) -> p t o", o=1).to_broadcast([P, NT, D]),
                                ALU.mult).then_inc(s_guf, 1)

            def hidden_reciprocal(bt):
                if not bt.there():
                    return
                dve.wait_ge(s_ge, bt.count(2, 2))
                v.reciprocal(GR[:, :, :], GP[:, :, :]).then_inc(s_h, 1)

            def hidden_gate(bt):
                if not bt.there():
                    return
                dve.wait_ge(s_h, bt.count(3, 1))
                v.tensor_tensor(GS[:, :, :], GUF[:, :, 0, :], GR[:, :, :], ALU.mult).then_inc(s_h, 1)

            def hidden_product(bt):
                if not bt.there():
                    return
                dve.wait_ge(s_h, bt.count(3, 2))
                if (due := bt.by(-1).count(2, 2)) is not None:
                    dve.wait_ge(s_h16, due)
                v.tensor_tensor(HF[:, :, :], GS[:, :, :], GUF[:, :, 1, :], ALU.mult).then_inc(s_h, 1)

            def out_turn(bt, half):
                if not bt.there():
                    return
                if half == 0:
                    if (due := bt.by(-1).count(3, 2)) is not None:
                        dve.wait_ge(s_on, due)
                dve.wait_ge(s_pv_full, bt.count(2, half + 1))
                v.transpose(OT[:, 2 * half:2 * half + 2, :, :].rearrange("p g b r -> p (g b r)"),
                            PO[:, :]).then_inc(s_ot, 1)

            def out_norm(bt):
                if not bt.there():
                    return
                dve.wait_ge(s_ot, bt.count(2, 2))
                v.reciprocal(RD[:, :, :], OT[:, :, :, C]).then_inc(s_on, 1)

            def out_scale(bt):
                if not bt.there():
                    return
                dve.wait_ge(s_on, bt.count(3, 1))
                v.tensor_tensor(ON[:, :, :, :].rearrange("p b g c -> p g b c"), OT[:, :, :, 0:C],
                                RD[:, :, :].rearrange("p g (b o) -> p g b o", o=1).to_broadcast([P, NG, 8, C]),
                                ALU.mult).then_inc(s_on, 1)

            def out_back(bt):
                if not bt.there():
                    return
                dve.wait_ge(s_on, bt.count(3, 2))
                if (due := bt.by(-1).count(2, 2)) is not None:
                    dve.wait_ge(s_oc16, due)
                v.transpose(OC[:, :], ON[:, :, :, :].rearrange("p b g c -> p (b g c)")).then_inc(s_on, 1)

            def values(bt):
                if not bt.there():
                    return
                if bt.fixed and bt.b < 2:
                    dve.wait_ge(s_ones, 2)
                    dve.wait_ge(s_cst, 96)
                dve.wait_ge(s_v_full, bt.count(1, 1))
                if (due := bt.by(-2).count(2, 2)) is not None:
                    dve.wait_ge(s_pv_full, due)
                v.tensor_tensor(VS[bt.par][:, :, :, 0:C],
                                BC[:, 0:NT * D].rearrange("p (t h c) -> p t h c", t=NT, c=C),
                                BR[:, 0:1, :].rearrange("p o (h c) -> p o h c", c=C)
                                .to_broadcast([P, NT, NH, C]), ALU.add).then_inc(s_v, 1)

            def maxima(bt, n):
                if not bt.there():
                    return
                lb, rt = n // 2, n % 2
                if n == 0:
                    if (due := bt.by(-1).count(1, 1)) is not None:
                        dve.wait_ge(s_mxc, due)
                dve.wait_ge(s_mx_full, bt.count(NCH, n + 1))
                v.tensor_reduce(
                    MXR[:, rt, :].rearrange("p (j g b) -> p g j b", j=4, b=8)[:, :, :, lb],
                    MX[n % 2][:, :].rearrange("p (h l) -> p h l", l=QR), axis=AX_X, op=ALU.max,
                    apply_transpose=True).then_inc(s_tr, 1)

            def hidden_mask(bt):
                if not bt.there():
                    return
                dve.wait_ge(s_ht, bt.count(1, 1))
                dve.wait_ge(s_mk, bt.count(NE, NE))
                if (due := bt.by(-1).count(1, 1)) is not None:
                    dve.wait_ge(s_dn_full, due)
                for e2 in range(2):
                    q = slice(NI * e2, NI * e2 + NI)
                    mk = MK[q, :, :].rearrange("p (e two) l -> p e two l", two=2)[:, :, e2, :]
                    for s in range(2):
                        last = v.tensor_tensor(HM[q, s, :, :],
                                               HT[q, s:s + 1, :].to_broadcast([NI, NE // 2, L]),
                                               mk, ALU.mult)
                    last.then_inc(s_hm, 1)

            def attended(bt):
                if not bt.there():
                    return
                dve.wait_ge(s_wo_full, bt.count(1, 1))
                dve.wait_ge(s_xbb, bt.count(1, 1))
                if (due := bt.by(-2).count(1, 1)) is not None:
                    dve.wait_ge(s_yf, due)
                v.tensor_tensor(X2[bt.par][:, :, :], BB[:, 0:NT * D].rearrange("p (t d) -> p t d", t=NT),
                                XBB[:, :, :], ALU.add).then_inc(s_x2, 1)

            def ln2_stats(bt):
                if not bt.there():
                    return
                if (due := bt.by(-1).count(4, 4)) is not None:
                    dve.wait_ge(s_ln2, due)
                dve.wait_ge(s_x2, bt.count(1, 1))
                for t in range(NT):
                    v.bn_stats(ST2[:, t, :], X2[bt.par][:, t, :]).then_inc(s_ln2, 1)

            def ln2_aggregate(bt):
                if not bt.there():
                    return
                if (due := bt.by(-1).count(2, 2)) is not None:
                    dve.wait_ge(s_x2f, due)
                dve.wait_ge(s_ln2, bt.count(4, 2))
                apart(dve, bt)
                for t in range(NT):
                    v.bn_aggr(MV2[:, t, :], ST2[:, t, :]).then_inc(s_ln2, 1)

            def result(bt):
                if not bt.there():
                    return
                dve.wait_ge(s_dn_full, bt.count(1, 1))
                prev = Batch(bt.trip, bt.off - 2)
                if (due := prev.half(16, 16)) is not None:
                    dve.wait_ge(s_y[prev.par], due)
                v.tensor_tensor(Y[bt.par][:, :, :], BB[:, 0:NT * D].rearrange("p (t d) -> p t d", t=NT),
                                X2[bt.par][:, :, :], ALU.add).then_inc(s_yf, 1)

            def logits_max(bt):
                if not bt.there():
                    return
                dve.wait_ge(s_lg_full, bt.count(1, 1))
                if (due := bt.by(-1).count(2, 1)) is not None:
                    dve.wait_ge(s_rex, due)
                v.tensor_reduce(LMX[:, :], BB[:, 0:NT * NE].rearrange("p (t e) -> p t e", t=NT), axis=AX_X,
                                op=ALU.max).then_inc(s_gate, 1)

            def logits_less(bt):
                if not bt.there():
                    return
                dve.wait_ge(s_gate, bt.count(4, 1))
                v.tensor_tensor(LLT[:, :, :], BB[:, 0:NT * NE].rearrange("p (t e) -> p t e", t=NT),
                                LMX[:, :].rearrange("p (t o) -> p t o", o=1).to_broadcast([P, NT, NE]),
                                ALU.is_lt).then_inc(s_gate, 1)

            def logits_number(bt):
                if not bt.there():
                    return
                dve.wait_ge(s_gate, bt.count(4, 2))
                v.scalar_tensor_tensor(LIX[:, :, :], LLT[:, :, :], float(NE), IOTA[:, :, :],
                                       ALU.mult, ALU.add).then_inc(s_gate, 1)

            def logits_first(bt):
                if not bt.there():
                    return
                dve.wait_ge(s_gate, bt.count(4, 3))
                if (due := bt.by(-1).count(1, 1)) is not None:
                    dve.wait_ge(s_eid_full, due)
                v.tensor_reduce(LID[:, :], LIX[:, :, :], axis=AX_X, op=ALU.min).then_inc(s_gate, 1)

            def weight(bt):
                if not bt.there():
                    return
                dve.wait_ge(s_rex, bt.count(2, 2))
                if (due := bt.by(-1).count(1, 1)) is not None:
                    dve.wait_ge(s_guf, due)
                v.reciprocal(RW[:, :], RP1[:, :]).then_inc(s_rw, 1)

            def max_join(bt):
                if not bt.there():
                    return
                dve.wait_ge(s_tr, bt.count(NCH, NCH))
                if (due := bt.by(-1).count(1, 1)) is not None:
                    dve.wait_ge(s_mt_full, due)
                v.tensor_tensor(MXC[:, :], MXR[:, 0, :], MXR[:, 1, :], ALU.max).then_inc(s_mxc, 1)

            def max_cut(bt):
                if not bt.there():
                    return
                dve.wait_ge(s_mt_full, bt.count(1, 1))
                if (due := bt.by(-1).count(2, 2)) is not None:
                    dve.wait_ge(s_m16, due)
                v.tensor_reduce(MN[:, :], BA[:, 0:P].rearrange("p (q l) -> p l q", q=4), axis=AX_X,
                                op=ALU.max).then_inc(s_m16, 1)

            def max_scale(bt):
                if not bt.there():
                    return
                dve.wait_ge(s_m16, bt.count(2, 1))
                if (due := bt.by(-1).half(64, 64)) is not None:
                    dve.wait_ge(s_m[1 - bt.par], due)
                v.tensor_scalar(M16[:, :], MN[:, :], -1.0 / MSCALE, None, ALU.mult).then_inc(s_m16, 1)

            def masks(bt):
                if not bt.there():
                    return
                dve.wait_ge(s_eid, bt.count(1, 1))
                if (due := bt.by(-1).count(2, 2)) is not None:
                    dve.wait_ge(s_hm, due)
                if (due := bt.by(-1).count(2, 2)) is not None:
                    dve.wait_ge(s_xm, due)
                for e in range(NE):
                    v.tensor_scalar(MK[:, e, :], EID[:, :], float(e), None, ALU.is_equal).then_inc(s_mk, 1)

            def rows_mask(bt, half):
                if not bt.there():
                    return
                if half == 0:
                    if (due := bt.by(-1).count(1, 1)) is not None:
                        dve.wait_ge(s_gu_full, due)
                dve.wait_ge(s_x2t, bt.count(1, 1))
                dve.wait_ge(s_mk, bt.count(NE, 4 * half + 4))
                e = slice(4 * half, 4 * half + 4)
                for s in range(2):
                    last = v.tensor_tensor(XM[:, s, e, :], X2T[:, s:s + 1, :].to_broadcast([P, 4, L]),
                                           MK[:, e, :], ALU.mult)
                last.then_inc(s_xm, 1)

            v.memset(Z[0][:], 0.0).then_inc(s_zero, 1)

            def step_all(trip, u):
                i2, i1, i0, m1, m2 = [Batch(trip, u + k) for k in (2, 1, 0, -1, -2)]
                logits_less(m2)
                maxima(i0, 14)
                logits_number(m2)
                maxima(i0, 15)
                logits_first(m2)
                max_join(i0)
                max_cut(i0)
                max_scale(i0)
                ln1_stats(i2)
                masks(m2)
                out_turn(m1, 0)
                rows_mask(m2, 0)
                rows_mask(m2, 1)
                ln1_aggregate(i2)
                out_turn(m1, 1)
                out_norm(m1)
                out_scale(m1)
                values(i1)
                weight(m2)
                out_back(m1)
                norm1(i2)
                gates_scale(m2)
                maxima(i1, 0)
                maxima(i1, 1)
                hidden_reciprocal(m2)
                maxima(i1, 2)
                hidden_gate(m2)
                maxima(i1, 3)
                hidden_product(m2)
                attended(m1)
                maxima(i1, 4)
                ln2_stats(m1)
                maxima(i1, 5)
                ln2_aggregate(m1)
                maxima(i1, 6)
                maxima(i1, 7)
                norm2(m1)
                maxima(i1, 8)
                maxima(i1, 9)
                hidden_mask(m2)
                maxima(i1, 10)
                maxima(i1, 11)
                result(m2)
                maxima(i1, 12)
                maxima(i1, 13)
                logits_max(m1)

            run(dve, step_all)

        @block.gpsimd
        def _(pool):
            g = nc.gpsimd

            def cut(bt, hi, lo, src, done, per, k):
                apart(pool, bt)
                g.tensor_scalar(hi, src, 1.0, 0.0, ALU.mult, ALU.add).then_inc(done, 1)
                pool.wait_ge(done, bt.count(per, k + 1))
                g.tensor_tensor(lo, src, hi, ALU.subtract).then_inc(done, 1)

            def rstd1(bt):
                if not bt.there():
                    return
                if (due := bt.by(-1).count(2, 2)) is not None:
                    pool.wait_ge(s_rs1, due)
                pool.wait_ge(s_ln1, bt.count(4, 4))
                apart(pool, bt)
                g.tensor_scalar(VE1[:, :, :], MV1[:, :, 1:2], EPS, None, ALU.add).then_inc(s_rs1, 1)
                pool.wait_ge(s_rs1, bt.count(2, 1))
                g.tensor_tensor(RS1[:, :, :], VE1[:, :, :], HALF[:, :, :], ALU.pow).then_inc(s_rs1, 1)

            def rstd2(bt):
                if not bt.there():
                    return
                if (due := bt.by(-1).count(2, 2)) is not None:
                    pool.wait_ge(s_rs2, due)
                pool.wait_ge(s_ln2, bt.count(4, 4))
                apart(pool, bt)
                g.tensor_scalar(VE2[:, :, :], MV2[:, :, 1:2], EPS, None, ALU.add).then_inc(s_rs2, 1)
                pool.wait_ge(s_rs2, bt.count(2, 1))
                g.tensor_tensor(RS2[:, :, :], VE2[:, :, :], HALF[:, :, :], ALU.pow).then_inc(s_rs2, 1)

            def rows1(bt):
                if not bt.there():
                    return
                pool.wait_ge(s_xnf, bt.count(2, 2))
                if (due := bt.by(-1).count(1, 1)) is not None:
                    pool.wait_ge(s_xt_full, due)
                cut(bt, XN[:, 0, :, :], XN[:, 1, :, :], XNF[:, :, :], s_xn, 2, 0)

            def rows2(bt):
                if not bt.there():
                    return
                pool.wait_ge(s_x2f, bt.count(2, 2))
                if (due := bt.by(-1).count(1, 1)) is not None:
                    pool.wait_ge(s_x2t_full, due)
                cut(bt, X2N[:, 0, :, :], X2N[:, 1, :, :], X2F[:, :, :], s_x2n, 2, 0)

            def stack_queries(bt):
                if not bt.there():
                    return
                g.memset(STILL[:, :], 0.0).then_inc(s_still, 1)
                if bt.fixed and bt.b < 2:
                    pool.wait_ge(s_zero, 2 * bt.b + 1)
                if (due := bt.by(-2).count(NCH, NCH)) is not None:
                    pool.wait_ge(s_sc_full, due)
                pool.wait_ge(s_qd, bt.count(2, 2))
                pool.wait_ge(s_still, bt.count(1, 1))
                apart(pool, bt)
                for j in range(4):
                    q = slice(32 * j, 32 * j + 32)
                    g.tensor_scalar(Z[bt.par][q, j, :, :], QD[q, :, :], 1.0, 0.0,
                                    ALU.mult, ALU.add).then_inc(s_z, 1)
                    pool.wait_ge(s_z, bt.count(4, j + 1))
                    apart(pool, bt)

            def residual(bt):
                if not bt.there():
                    return
                if bt.fixed and bt.b == 0:
                    pool.wait_ge(s_cst, 96)
                if (due := bt.by(-1).count(1, 1)) is not None:
                    pool.wait_ge(s_x2, due)
                pool.wait_ge(s_xb[bt.par], bt.half(16, 16))
                g.tensor_tensor(XBB[:, :, :], XB[bt.par][:, :, :], BR[:, 1:2, :].to_broadcast([P, NT, D]),
                                ALU.add).then_inc(s_xbb, 1)

            def hidden(bt):
                if not bt.there():
                    return
                pool.wait_ge(s_h, bt.count(3, 3))
                if (due := bt.by(-1).count(1, 1)) is not None:
                    pool.wait_ge(s_ht_full, due)
                src = HF[:, :, :].rearrange("p t (o i) -> p t o i", o=1).to_broadcast([P, NT, 2, NI])
                cut(bt, H16[:, 0, :, :, :], H16[:, 1, :, :, :], src, s_h16, 2, 0)

            def attention(bt):
                if not bt.there():
                    return
                pool.wait_ge(s_on, bt.count(3, 3))
                if (due := bt.by(-1).count(1, 1)) is not None:
                    pool.wait_ge(s_wo_full, due)
                cut(bt, OC16[:, 0, :], OC16[:, 1, :], OC[:, :], s_oc16, 2, 0)

            def qk(bt):
                if not bt.there():
                    return
                pool.wait_ge(s_qk, bt.count(3, 3))
                if (due := bt.by(-1).count(2, 2)) is not None:
                    pool.wait_ge(s_selk_full, due)
                if (due := bt.by(-1).count(1, 1)) is not None:
                    pool.wait_ge(s_self_full, due)
                if (due := bt.by(-1).count(2, 2)) is not None:
                    pool.wait_ge(s_selq_full, due)
                cut(bt, QK16[:, 0, :], QK16[:, 1, :], QKF[:, :], s_qk16, 2, 0)

            g.memset(WARM[:, :], 0.0).then_inc(s_warm, 1)
            g.memset(HALF[:, :, :], -0.5).then_inc(s_half, 1)
            pool.wait_ge(s_half, 1)
            for p in range(2):
                g.memset(VS[p][:], 1.0).then_inc(s_ones, 1)

            def step_all(trip, u):
                i2, i1, i0, m1, m2 = [Batch(trip, u + k) for k in (2, 1, 0, -1, -2)]
                stack_queries(i1)
                residual(m1)
                rstd1(i2)
                attention(m1)
                rows1(i2)
                hidden(m2)
                rstd2(m1)
                rows2(m1)
                qk(i2)

            run(pool, step_all)


def kernel(L0_attn_hidden_states, L0_attn_Wq, L0_attn_bq, L0_attn_Wk, L0_attn_bk, L0_attn_Wv, L0_attn_bv,
           L0_attn_Wo, L0_attn_bo, L0_attn_dist_emb, L0_ffn_gate_w, L0_ffn_w_gate, L0_ffn_w_up, L0_ffn_w_down):
    import numpy as np
    import concourse.bacc as bacc
    from concourse.bass_utils import run_bass_kernel_spmd

    a = {k: np.asarray(v) for k, v in dict(
        x=L0_attn_hidden_states, wq=L0_attn_Wq, bq=L0_attn_bq, wk=L0_attn_Wk, bk=L0_attn_bk, wv=L0_attn_Wv,
        bv=L0_attn_bv, wo=L0_attn_Wo, bo=L0_attn_bo, dist=L0_attn_dist_emb, gw=L0_ffn_gate_w,
        wg=L0_ffn_w_gate, wu=L0_ffn_w_up, wd=L0_ffn_w_down).items()}

    wo_rows = a["wo"].T.reshape(NG, 4, C, D).transpose(1, 0, 2, 3).reshape(D, D)
    gu = np.stack([a["wg"], a["wu"]], 1).transpose(3, 0, 1, 2).reshape(D, NE * 2 * NI)
    wd = a["wd"].reshape(NE // 2, 2, D, NI).transpose(1, 3, 0, 2).reshape(2 * NI, (NE // 2) * D)
    w_all = np.concatenate([a["wq"].T, a["wk"].T, a["wv"].T, wo_rows, a["gw"].T, gu, wd], axis=1)
    biases = np.stack([a["bq"], a["bk"]], 1)
    edges = np.tile(a["dist"][[LEFT + RIGHT, 0]].T, (NH, 1))
    b_rows = np.broadcast_to(np.stack([a["bv"], a["bo"]])[None], (P, 2, D))
    at = np.clip(np.arange(TZW)[None, :] - XOFF - np.arange(4)[:, None], -LEFT, RIGHT) + LEFT
    dist_t = np.zeros((4, 4, C, TZW), a["dist"].dtype)
    dist_t[:, 0:3] = a["dist"][at].transpose(0, 2, 1)[:, None]
    dist0 = np.zeros((4, 4, C, 1), a["dist"].dtype)
    dist0[:, 0:3] = a["dist"][0][None, None, :, None]

    sel = np.zeros((NG, 4, C, 4, NG, 4, 4, C), np.float16)
    for g in range(NG):
        for j in range(4):
            for c in range(C):
                for operand, rows in ((0, (0, 1)), (1, (2,)), (2, (0, 2)), (3, (1,))):
                    for row in rows:
                        sel[g, j, c, operand, g, j, row, c] = 1
    kbias = np.zeros((4, 4, C, 1), np.float32)
    kbias[:, 3, 0] = MSCALE
    restrow = np.zeros((4, 4, C, 1), np.float32)
    restrow[:, 1] = -1
    iota = np.broadcast_to(np.arange(NE, dtype=np.float32), (P, NT, NE))
    arrays = {
        "x": a["x"], "w_all": w_all, "biases": biases, "edges": edges, "b_rows": b_rows,
        "dist_t": dist_t.reshape(P, TZW), "dist0": dist0.reshape(P, 1),
        "ident16": np.eye(P, dtype=np.float16), "ident32": np.eye(P, dtype=np.float32),
        "sel": sel.reshape(P, 4, NG, P), "kbias": kbias.reshape(P, 1), "restrow": restrow.reshape(P, 1),
        "iota": iota,
    }
    arrays = {k: np.ascontiguousarray(v) for k, v in arrays.items()}

    nc = bacc.Bacc("TRN2", target_bir_lowering=False, num_devices=1)
    args = [nc.dram_tensor(f"in_{k}", v.shape, mybir.dt.from_np(v.dtype), kind="ExternalInput").ap()
            for k, v in arrays.items()]
    out = nc.dram_tensor("out_0", (NB, L, D), F32, kind="ExternalOutput").ap()
    turned_q = nc.dram_tensor("turned_q", (2, 4, P, NG * L // 4), F16, kind="Internal").ap()
    build(nc, *args, turned_q, out)
    r = run_bass_kernel_spmd(nc, [{f"in_{k}": v for k, v in arrays.items()}], core_ids=[0])
    return r.results[0]["out_0"]
```
